# Optimizing a Trainium2 kernel written in Bass

```python
import numpy as np
import jax
import jax.numpy as jnp

def _softmax(x, axis=-1):
    return jax.nn.softmax(x, axis=axis)

def _gelu(x):
    return jax.nn.gelu(x, approximate=True)

def _silu(x):
    return jax.nn.silu(x)

def _sigmoid(x):
    return jax.nn.sigmoid(x)

def _layernorm(x, axis=-1, eps=1e-05):
    m = jnp.mean(x, axis=axis, keepdims=True)
    v = jnp.var(x, axis=axis, keepdims=True)
    return (x - m) / jnp.sqrt(v + eps)

def _scatter_add(tgt, idx, src, axis=0):
    return tgt.at[idx].add(src)

def _segment_sum(src, seg, n):
    return jax.ops.segment_sum(src, seg, n)
kernel_name = 'mk_perceiver_d1_seqx_r4_1a2707'

def setup_inputs(seed: int=0):
    np.random.seed(seed)
    _w = jnp.asarray

    def _rec_inputs():
        import jax
        import jax.numpy as jnp
        _rk = jax.random.key(seed)
        x = -0.0002928 + 1 * jax.random.normal(jax.random.fold_in(_rk, 1), (4, 256, 256), jnp.float32)
        _lenS = 256 - jax.random.randint(jax.random.fold_in(_rk, 7), (4,), 0, max(1, 256 // 4) + 1, jnp.int32)
        _lenS2 = 4096 - jax.random.randint(jax.random.fold_in(_rk, 8), (4,), 0, max(1, 4096 // 4) + 1, jnp.int32)
        _ctx_768P = jax.random.normal(jax.random.fold_in(_rk, 11), (4, 16, 192), jnp.float32)
        _ctx_768c = jax.random.dirichlet(jax.random.fold_in(_rk, 511), 0.3 * jnp.ones((16,), jnp.float32), (4, 4096))
        _ctx_768t = jnp.einsum('bsk,bkd->bsd', _ctx_768c, _ctx_768P)
        _ctx_768t = _ctx_768t * jax.lax.rsqrt(jnp.mean(jnp.square(_ctx_768t)) + 1e-12) * 0.953939
        ctx_768 = 2.09791e-05 + 1.00001 * (_ctx_768t + 0.3 * jax.random.normal(jax.random.fold_in(_rk, 611), (4, 4096, 192), jnp.float32))
        return (x, ctx_768)
    x, ctx_768 = _rec_inputs()

    def _L0_xattn_setup():
        import jax, jax.numpy as jnp
        import numpy as np
        N_HEADS = 16
        EMBED_DIM = 256
        CROSS_DIM = 192
        HEAD_DIM = EMBED_DIM // N_HEADS
        key = jax.random.key(seed)
        ks = jax.random.split(key, 12)
        B, SQ, SKV = (2, 512, 512)
        s_in = 1.0 / np.sqrt(EMBED_DIM)
        s_cross = 1.0 / np.sqrt(CROSS_DIM)
        return {'x': jax.random.normal(ks[0], (B, SQ, EMBED_DIM), jnp.float32), 'y': jax.random.normal(ks[1], (B, SKV, CROSS_DIM), jnp.float32), 'wq': jax.random.normal(ks[2], (EMBED_DIM, EMBED_DIM), jnp.float32) * s_in, 'bq': jax.random.normal(ks[3], (EMBED_DIM,), jnp.float32) * s_in, 'wk': jax.random.normal(ks[4], (EMBED_DIM, CROSS_DIM), jnp.float32) * s_cross, 'bk': jax.random.normal(ks[5], (EMBED_DIM,), jnp.float32) * s_cross, 'wv': jax.random.normal(ks[6], (EMBED_DIM, CROSS_DIM), jnp.float32) * s_cross, 'bv': jax.random.normal(ks[7], (EMBED_DIM,), jnp.float32) * s_cross, 'wo': jax.random.normal(ks[8], (EMBED_DIM, EMBED_DIM), jnp.float32) * s_in, 'bo': jax.random.normal(ks[9], (EMBED_DIM,), jnp.float32) * s_in}
    _L0_xattn_all = _L0_xattn_setup()
    _L0_xattn_in = {k: v for k, v in _L0_xattn_all.items() if k in ('wq', 'bq', 'wk', 'bk', 'wv', 'bv', 'wo', 'bo')}
    del _L0_xattn_all

    def _L0_attn_setup():
        import jax, jax.numpy as jnp
        import numpy as np
        B, L, D = (2, 512, 256)
        H = 16
        HD = D // H
        WINDOW = 64

        def _window_mask(seq_len, window_size, dtype):
            half = window_size // 2
            i = jnp.arange(seq_len)[:, None]
            j = jnp.arange(seq_len)[None, :]
            allowed = jnp.abs(i - j) <= half
            return jnp.where(allowed, jnp.zeros((), dtype), jnp.asarray(-jnp.inf, dtype))
        key = jax.random.key(seed)
        k1, k2, k3 = jax.random.split(key, 3)
        s = 0.02
        return {'x': jax.random.normal(k1, (B, L, D), dtype=jnp.float32), 'w_qkv': jax.random.normal(k2, (D, 3 * D), dtype=jnp.float32) * s, 'b_qkv': jnp.zeros((3 * D,), dtype=jnp.float32), 'w_out': jax.random.normal(k3, (D, D), dtype=jnp.float32) * s, 'b_out': jnp.zeros((D,), dtype=jnp.float32)}
    _L0_attn_all = _L0_attn_setup()
    _L0_attn_in = {k: v for k, v in _L0_attn_all.items() if k in ('w_qkv', 'b_qkv', 'w_out', 'b_out')}
    del _L0_attn_all

    def _L0_ffn_setup():
        import jax, jax.numpy as jnp
        import numpy as np
        D_MODEL = 256
        D_HIDDEN = 1024
        NUM_BANKS = 16
        NUM_SELECTED = 2
        key = jax.random.key(seed)
        ks = jax.random.split(key, 7)
        s = 0.02
        return {'tensor': jax.random.normal(ks[0], (4, 256, D_MODEL), dtype=jnp.float32), 'Wr': jax.random.normal(ks[1], (D_MODEL, NUM_BANKS), dtype=jnp.float32) * s, 'br': jnp.zeros((NUM_BANKS,), dtype=jnp.float32), 'W1': jax.random.normal(ks[2], (NUM_BANKS, D_MODEL, D_HIDDEN), dtype=jnp.float32) * s, 'b1': jnp.zeros((NUM_BANKS, D_HIDDEN), dtype=jnp.float32), 'W2': jax.random.normal(ks[3], (NUM_BANKS, D_HIDDEN, D_MODEL), dtype=jnp.float32) * s, 'b2': jnp.zeros((NUM_BANKS, D_MODEL), dtype=jnp.float32)}
    _L0_ffn_all = _L0_ffn_setup()
    _L0_ffn_in = {k: v for k, v in _L0_ffn_all.items() if k in ('Wr', 'br', 'W1', 'b1', 'W2', 'b2')}
    del _L0_ffn_all
    return {'x': x, 'ctx_768': ctx_768, 'L0_xattn_wq': _L0_xattn_in['wq'], 'L0_xattn_bq': _L0_xattn_in['bq'], 'L0_xattn_wk': _L0_xattn_in['wk'], 'L0_xattn_bk': _L0_xattn_in['bk'], 'L0_xattn_wv': _L0_xattn_in['wv'], 'L0_xattn_bv': _L0_xattn_in['bv'], 'L0_xattn_wo': _L0_xattn_in['wo'], 'L0_xattn_bo': _L0_xattn_in['bo'], 'L0_attn_w_qkv': _L0_attn_in['w_qkv'], 'L0_attn_b_qkv': _L0_attn_in['b_qkv'], 'L0_attn_w_out': _L0_attn_in['w_out'], 'L0_attn_b_out': _L0_attn_in['b_out'], 'L0_ffn_Wr': _L0_ffn_in['Wr'], 'L0_ffn_br': _L0_ffn_in['br'], 'L0_ffn_W1': _L0_ffn_in['W1'], 'L0_ffn_b1': _L0_ffn_in['b1'], 'L0_ffn_W2': _L0_ffn_in['W2'], 'L0_ffn_b2': _L0_ffn_in['b2']}

def reference(x, ctx_768, L0_xattn_wq, L0_xattn_bq, L0_xattn_wk, L0_xattn_bk, L0_xattn_wv, L0_xattn_bv, L0_xattn_wo, L0_xattn_bo, L0_attn_w_qkv, L0_attn_b_qkv, L0_attn_w_out, L0_attn_b_out, L0_ffn_Wr, L0_ffn_br, L0_ffn_W1, L0_ffn_b1, L0_ffn_W2, L0_ffn_b2):
    import jax
    import jax.numpy as jnp

    def _L0_xattn_ref(x, y, wq, bq, wk, bk, wv, bv, wo, bo):
        import jax, jax.numpy as jnp
        import numpy as np
        N_HEADS = 16
        EMBED_DIM = 256
        CROSS_DIM = 192
        HEAD_DIM = EMBED_DIM // N_HEADS
        B, SQ, E = x.shape
        q = x @ wq.T + bq
        k = y @ wk.T + bk
        v = y @ wv.T + bv
        q = q.reshape(B, SQ, N_HEADS, HEAD_DIM).transpose(0, 2, 1, 3)
        k = k.reshape(B, -1, N_HEADS, HEAD_DIM).transpose(0, 2, 1, 3)
        v = v.reshape(B, -1, N_HEADS, HEAD_DIM).transpose(0, 2, 1, 3)
        scale = 1.0 / jnp.sqrt(jnp.asarray(HEAD_DIM, x.dtype))
        score = jnp.einsum('bhqd,bhkd->bhqk', q, k) * scale
        attn = jax.nn.softmax(score, axis=-1)
        out = jnp.einsum('bhqk,bhkd->bhqd', attn, v)
        out = out.transpose(0, 2, 1, 3).reshape(B, SQ, E)
        return out @ wo.T + bo

    def _L0_attn_ref(x, w_qkv, b_qkv, w_out, b_out):
        import jax, jax.numpy as jnp
        import numpy as np
        B, L, D = (2, 512, 256)
        H = 16
        HD = D // H
        WINDOW = 64

        def _window_mask(seq_len, window_size, dtype):
            half = window_size // 2
            i = jnp.arange(seq_len)[:, None]
            j = jnp.arange(seq_len)[None, :]
            allowed = jnp.abs(i - j) <= half
            return jnp.where(allowed, jnp.zeros((), dtype), jnp.asarray(-jnp.inf, dtype))
        b, l, d = x.shape
        qkv = x @ w_qkv + b_qkv
        qkv = qkv.reshape(b, l, 3, H, HD)
        q = jnp.transpose(qkv[:, :, 0], (0, 2, 1, 3))
        k = jnp.transpose(qkv[:, :, 1], (0, 2, 1, 3))
        v = jnp.transpose(qkv[:, :, 2], (0, 2, 1, 3))
        scale = 1.0 / np.sqrt(HD)
        scores = jnp.einsum('bhqd,bhkd->bhqk', q, k) * scale
        scores = scores + _window_mask(l, WINDOW, scores.dtype)[None, None]
        attn = jax.nn.softmax(scores, axis=-1)
        out = jnp.einsum('bhqk,bhkd->bhqd', attn, v)
        out = jnp.transpose(out, (0, 2, 1, 3)).reshape(b, l, d)
        return out @ w_out + b_out

    def _L0_ffn_ref(tensor, Wr, br, W1, b1, W2, b2):
        import jax, jax.numpy as jnp
        import numpy as np
        D_MODEL = 256
        D_HIDDEN = 1024
        NUM_BANKS = 16
        NUM_SELECTED = 2
        logits = jnp.einsum('bsd,de->bse', tensor, Wr) + br
        probs = jax.nn.softmax(logits, axis=-1)
        topv, topi = jax.lax.top_k(probs, NUM_SELECTED)
        gate = jnp.sum(jax.nn.one_hot(topi, NUM_BANKS, dtype=tensor.dtype) * topv[..., None], axis=-2)
        h = jax.nn.relu(jnp.einsum('bsd,edh->bseh', tensor, W1) + b1)
        y = jnp.einsum('bseh,ehm->bsem', h, W2) + b2
        out = jnp.einsum('bse,bsem->bsm', gate, y)
        return out
    x = x + _L0_xattn_ref(_layernorm(x, axis=-1), ctx_768, L0_xattn_wq, L0_xattn_bq, L0_xattn_wk, L0_xattn_bk, L0_xattn_wv, L0_xattn_bv, L0_xattn_wo, L0_xattn_bo)
    x = x + _L0_attn_ref(_layernorm(x, axis=-1), L0_attn_w_qkv, L0_attn_b_qkv, L0_attn_w_out, L0_attn_b_out)
    x = x + _L0_ffn_ref(_layernorm(x, axis=-1), L0_ffn_Wr, L0_ffn_br, L0_ffn_W1, L0_ffn_b1, L0_ffn_W2, L0_ffn_b2)
    return x

_drawn_inputs = setup_inputs


def setup_inputs(seed=0):
    import zlib

    import numpy as np

    out = dict(_drawn_inputs(seed))
    spreads = {'L0_attn_b_qkv': (0.0, 0.292),
     'L0_attn_b_out': (0.0, 0.1),
     'L0_ffn_br': (0.0, 0.525),
     'L0_ffn_b1': (0.0, 0.8),
     'L0_ffn_b2': (0.0, 0.618)}
    factors = {'L0_xattn_bq': 4.875,
     'L0_xattn_bk': 8.0,
     'L0_ffn_Wr': 2.726,
     'L0_ffn_W1': 3.652,
     'L0_ffn_W2': 2.954}
    for name, (base, spread) in spreads.items():
        noise = np.random.default_rng([zlib.crc32(name.encode()), seed]).standard_normal(out[name].shape)
        drawn = base * np.exp(spread * noise) if base else spread * noise
        out[name] = jnp.asarray(drawn.astype(out[name].dtype))
    for name, factor in factors.items():
        out[name] = (out[name] * factor).astype(out[name].dtype)
    return out
```

```python
from contextlib import ExitStack

import numpy as np

import concourse.bass as bass
from concourse import mybir

F32 = mybir.dt.float32
BF16 = mybir.dt.bfloat16
U32 = mybir.dt.uint32
ACT = mybir.ActivationFunctionType
ALU = mybir.AluOpType
AX_X = mybir.AxisListType.X

P = 128
BATCH, SEQ, EMB = 4, 256, 256
KV, CTX = 4096, 192
HEADS, HD = 16, 16
TOK = BATCH * SEQ
TT = TOK // P
KE = EMB // P
KC = CTX // 2
GH = 4
GROUPS = BATCH * HEADS // GH
NG = HEADS // GH
KT = KV // P
CH = 512
NCH = KV // CH
VW = HD + 1
SLOTS = 6
K_PART = (0, 0, 0, 1, 1, 2)
Q_PART = (0, 1, 2, 0, 1, 0)
STK = SLOTS * HD
ROWS = STK + 3
QSCALE = 1.0 / HD ** 0.5
EPS = 1e-5
HALF = 32
WIN = P + HALF
BANKS, HID, NSEL = 16, 1024, 2
HC = HID // P


class Counter:

    def __init__(self, sem):
        self.sem, self.value = sem, 0


def build(nc, a, out, scratch):
    ctx = ExitStack()
    with ctx:
        def counter(name):
            return Counter(ctx.enter_context(nc.semaphore(name)))

        queue = {n: [] for n in ("pe", "act", "dve", "pool", "sp")}
        waited = {n: {} for n in queue}
        every = []

        def put(engine, make, sem, after=(), by=1):
            waits = []
            for c, v in after:
                if waited[engine].get(c, 0) < v:
                    waited[engine][c] = v
                    waits.append((c.sem, v))
            if sem is not None:
                sem.value += by
                if sem not in every:
                    every.append(sem)
            queue[engine].append((waits, make, sem.sem if sem else None, by))
            return (sem, sem.value) if sem else None

        def dma(engine, dst, src, sem, after=()):
            return put(engine, lambda e, d=dst, s=src: e.dma_start(d, s), sem, after, 16)

        def phase_end():
            return [(c, c.value) for c in every]

        arena = ctx.enter_context(nc.sbuf_tensor("arena", [P, 52600], F32))
        top = [0]

        def carve(shape, dt=F32):
            n = int(np.prod(shape)) * (2 if dt == BF16 else 4)
            n = (n + 3) // 4
            v = arena[:, top[0]:top[0] + n]
            top[0] += n
            assert top[0] <= 52600, top[0]
            if dt != F32:
                v = v.bitcast(dt)
            if len(shape) == 2:
                v = v.rearrange("p (a b) -> p a b", a=shape[0])
            elif len(shape) == 3:
                v = v.rearrange("p (a b c) -> p a b c", a=shape[0], b=shape[1])
            return v

        psum = ctx.enter_context(nc.psum_tensor("psum", [P, 8 * 512], F32))

        def bank(i, n=1):
            return psum[:, i * 512:(i + n) * 512]

        x = carve((TT, EMB))
        identf = carve((P,))
        identb = carve((P,), BF16)
        lsel = carve((P,))
        stats = carve((TT, 6))
        mv = carve((TT, 2))
        rstd = carve((TT,))
        rtmp = carve((2, TT))
        o_raw = carve((SEQ,))
        o_rl = carve((SEQ,))
        o_norm = carve((NG, SEQ))
        kept = top[0]

        ld_const = counter("ld_const")
        dve_ln = counter("dve_ln")
        pe_lnT = counter("pe_lnT")
        act_lnT = counter("act_lnT")
        act_ln = counter("act_ln")

        dma("sp", x, a["x"], ld_const)
        for dst, src in ((identf, "identf"), (lsel, "lsel")):
            t_const = dma("sp", dst, a[src], ld_const)
        t_identb = put("dve", lambda e: e.tensor_copy(identb, identf), dve_ln, [t_const])

        def layernorm_T(xT, xn, after, banks):
            for i in range(TT):
                put("dve", lambda e, i=i: e.bn_stats(stats[:, i, :], x[:, i, :]), dve_ln, after)
            t = (dve_ln, dve_ln.value)
            for i in range(TT):
                t2 = put("dve", lambda e, i=i: e.bn_aggr(mv[:, i, :], stats[:, i, :]), dve_ln, [t])
            var = rtmp[:, 0, :]
            t = put("dve", lambda e: e.tensor_scalar_add(var, mv[:, :, 1], EPS), dve_ln, [t2])
            t = put("act", lambda e: e.activation(rstd, var, ACT.Ln), act_ln, [t])
            t = put("act", lambda e: e.activation(rstd, rstd, ACT.Exp, scale=-0.5), act_ln, [t])
            sq = rtmp[:, 1, :]
            for _ in range(2):
                t = put("dve", lambda e: e.tensor_tensor(sq, rstd, rstd, ALU.mult), dve_ln, [t])
                t = put("dve", lambda e: e.tensor_tensor(sq, sq, var, ALU.mult), dve_ln, [t])
                t = put("dve", lambda e: e.tensor_scalar(sq, sq, -0.5, 1.5, ALU.mult, ALU.add), dve_ln, [t])
                t = put("dve", lambda e: e.tensor_tensor(rstd, rstd, sq, ALU.mult), dve_ln, [t])
            norm = []
            for i in range(TT):
                norm.append(put("dve", lambda e, i=i: e.tensor_scalar(
                    xn[:, i, :], x[:, i, :], mv[:, i, 0:1], rstd[:, i:i + 1], ALU.subtract, ALU.mult), dve_ln, [t]))
            done, n = [], 0
            evac = [None] * 2
            for k in range(KE):
                for half in range(TT // 4):
                    dst = bank(banks[n % 2])
                    for j in range(4):
                        i = 4 * half + j
                        w = [norm[i], t_const] + ([evac[n % 2]] if evac[n % 2] else [])
                        t = put("pe", lambda e, i=i, j=j, k=k, dst=dst: e.matmul(
                            dst[:, j * P:(j + 1) * P], xn[:, i, k * P:(k + 1) * P], identf, start=True, stop=True),
                            pe_lnT, w)
                    evac[n % 2] = put("act", lambda e, k=k, half=half, dst=dst: e.activation(
                        xT[:, k, half * CH:(half + 1) * CH], dst, ACT.Copy), act_lnT, [t])
                    done.append(evac[n % 2])
                    n += 1
            return done[-1]

        kstack = [carve((GH, KV), BF16) for _ in range(3)]
        setup_at = top[0]
        pieces = carve((3, KV), BF16)
        vals = carve((KT, HEADS * VW))
        ctx_in = [carve((2, CH)) for _ in range(2)]
        wts = [carve((GH * SEQ,)) for _ in range(2)]
        qstack = [carve((GH, SEQ), BF16) for _ in range(3)]
        rest = [carve((CH,)) for _ in range(2)]
        wk = carve((2, EMB))
        wv = carve((2, EMB))
        wo = carve((NG, EMB))
        bk = carve((KE,))
        bv = carve((NG,))
        bq = carve((KE,))
        part_max = carve((GH * 2, NCH))
        neg_max = carve((GH * 2,))
        neg_rest = carve((GH * 2,))
        neg_parts = carve((3, GH * 2), BF16)
        keep_top, top[0] = top[0], setup_at
        xn1 = carve((TT, EMB))
        xT1 = carve((KE, TOK))
        wq = carve((KE, EMB))
        qf = carve((KE, TOK))
        bo_bc = carve((EMB,))
        qparts = carve((3, KE, TOK), BF16)
        qrest = carve((CH,))
        top[0] = keep_top

        ld_w = counter("ld_w")
        dma("sp", wq, a["wqT"], ld_w)
        for dst, src in ((wk, "wkT"), (wv, "wvT")):
            dma("sp", dst[0:KC], a[src], ld_w)
        for dst, src in ((wo, "woT"), (bk, "bk"), (bv, "bv"), (bq, "bq"), (bo_bc, "bo")):
            t_w = dma("sp", dst, a[src], ld_w)

        pool_set = counter("pool_set")
        for s in range(3):
            t_ones = put("pool", lambda e, s=s: e.memset(kstack[s][STK:ROWS], 1.0), pool_set)
        dve_set = counter("dve_set")
        t_zero = put("dve", lambda e: e.memset(psum[:, :], 0.0), dve_set)

        t_xT = layernorm_T(xT1, xn1, [t_const, t_zero], (0, 1))
        pe_q, dve_q, act_q, st_q = counter("pe_q"), counter("dve_q"), counter("act_q"), counter("st_q")
        free = [None, None]
        for m in range(KE):
            for half in range(2):
                n = 2 * m + half
                dst = bank(2 + n % 2)
                for k in range(KE):
                    t = put("pe", lambda e, m=m, half=half, k=k, dst=dst: e.matmul(
                        dst, wq[:, k, m * P:(m + 1) * P], xT1[:, k, half * CH:(half + 1) * CH],
                        start=(k == 0), stop=(k == KE - 1)), pe_q, [t_xT, t_w] + [f for f in [free[n % 2]] if f])
                sl = slice(half * CH, (half + 1) * CH)
                free[n % 2] = t = put("dve", lambda e, m=m, sl=sl, dst=dst: e.tensor_scalar(
                    qf[:, m, sl], dst, bq[:, m:m + 1], QSCALE, ALU.add, ALU.mult), dve_q, [t])
                t = put("dve", lambda e, m=m, sl=sl: e.tensor_copy(qparts[:, 0, m, sl], qf[:, m, sl]), dve_q, [t])
                t = put("dve", lambda e, m=m, sl=sl: e.tensor_tensor(
                    qrest, qf[:, m, sl], qparts[:, 0, m, sl], ALU.subtract), dve_q, [t])
                t = put("dve", lambda e, m=m, sl=sl: e.tensor_copy(qparts[:, 1, m, sl], qrest), dve_q, [t])
                t = put("dve", lambda e, m=m, sl=sl: e.tensor_tensor(
                    qparts[:, 2, m, sl], qrest, qparts[:, 1, m, sl], ALU.subtract), dve_q, [t])
        qd = scratch["qparts"].rearrange("s (k p) t -> s p k t", p=P)
        for s in range(3):
            t_qd = dma("sp", qd[s], qparts[:, s], st_q, [t])
        for i in range(TT):
            t_bo = put("dve", lambda e, i=i: e.tensor_tensor(x[:, i, :], x[:, i, :], bo_bc, ALU.add), dve_q,
                       [t_w, (dve_ln, dve_ln.value)])
        setup_done = phase_end()

        t_vones = put("pool", lambda e: e.memset(vals.rearrange("p t (h w) -> p t h w", w=VW)[:, :, :, HD], 1.0),
                      pool_set, setup_done)

        S_BANKS = (0, 2)
        M_BANKS = (4, 5)
        X_BANK, O_BANK = 6, 7

        pe_proj, pe_score, pe_max, pe_pv, pe_end = (counter(n) for n in ("pe_proj", "pe_score", "pe_max", "pe_pv", "pe_end"))
        act_hi, act_exp, act_val = counter("act_hi"), counter("act_exp"), counter("act_val")
        dve_rest, dve_max, dve_end, dve_neg = (counter(n) for n in ("dve_rest", "dve_max", "dve_end", "dve_neg"))
        pool_part = counter("pool_part")
        ld_ctx = [counter(f"ld_ctx{i}") for i in range(2)]
        ld_k = [counter(f"ld_k{i}") for i in range(3)]
        ld_q = [counter(f"ld_q{i}") for i in range(3)]

        x_free = [None]
        ctx_used = [None, None]
        n_ctx = [0]
        ctx_now = [None]
        scores_done = {}
        exp_done = []
        pv_done = []
        max_used = [None, None]
        n_max = [0]
        pieces_read = [[]]
        pieces_ready = {}
        val_written = {}
        k_ready, q_ready, neg_ready = {}, {}, {}

        def opt(*t):
            return [v for v in t if v]

        def load_ctx(b, c):
            i = n_ctx[0] % 2
            n_ctx[0] += 1
            t = dma("sp", ctx_in[i][0:KC], a["ctxT"][b, :, :, c * CH:(c + 1) * CH], ld_ctx[i],
                    opt(ctx_used[i]) + setup_done)
            return i, t

        def load_q(g):
            b, hg = divmod(g, NG)
            after = opt(scores_done.get(g - 3)) + setup_done + [t_qd]
            for s in range(SLOTS):
                src = scratch["qparts"][Q_PART[s], hg * GH * HD:(hg + 1) * GH * HD, b * SEQ:(b + 1) * SEQ]
                t = dma("sp", qstack[g % 3][s * HD:(s + 1) * HD], src.rearrange("(h d) t -> d h t", d=HD),
                        ld_q[g % 3], after)
            q_ready[g] = t

        def scatter_k(g):
            after = opt(scores_done.get(g - 3), *pieces_ready[g // 2])
            for h in range(GH):
                row = ((g % 2) * GH + h) * HD
                for s in range(SLOTS):
                    t = dma("sp", kstack[g % 3][s * HD:(s + 1) * HD, h], pieces[row:row + HD, K_PART[s]],
                            ld_k[g % 3], after)
            k_ready[g] = t
            pieces_read[0] = opt(*pieces_read[0]) + [t]

        def project_k(mt, c):
            b, m = divmod(mt, 2)
            i, t_in = load_ctx(b, c)
            dst = bank(X_BANK)
            for k in range(2):
                t = put("pe", lambda e, k=k: e.matmul(dst, wk[0:KC, k, m * P:(m + 1) * P], ctx_in[i][0:KC, k],
                                                      start=(k == 0), stop=(k == 1)),
                        pe_proj, opt(t_in, t_w, x_free[0]))
            ctx_used[i] = t
            sl = slice(c * CH, (c + 1) * CH)
            hi = pieces[:, 0, sl]
            t_hi = put("act", lambda e: e.activation(hi, dst, ACT.Identity, bias=bk[:, m:m + 1]), act_hi,
                       [t] + pieces_read[0])
            r = rest[c % 2]
            t_r = put("dve", lambda e: e.scalar_tensor_tensor(r, dst, bk[:, m:m + 1], hi, ALU.add, ALU.subtract),
                      dve_rest, opt(t_hi, rest_used[c % 2]))
            x_free[0] = t_r
            t = put("pool", lambda e: e.tensor_copy(pieces[:, 1, sl], r), pool_part, [t_r] + pieces_read[0])
            t = put("pool", lambda e: e.tensor_tensor(pieces[:, 2, sl], r, pieces[:, 1, sl], ALU.subtract),
                    pool_part, [t])
            rest_used[c % 2] = t
            pieces_ready[mt] = [t_hi, t]

        rest_used = [None, None]

        def project_v(b, t_):
            c, j = divmod(t_, CH // P)
            if j == 0:
                ctx_now[0] = load_ctx(b, c)
            i, t_in = ctx_now[0]
            dst = bank(X_BANK)[:, 0:EMB]
            for k in range(2):
                t = put("pe", lambda e, k=k: e.matmul(dst, ctx_in[i][0:KC, k, j * P:(j + 1) * P], wv[0:KC, k],
                                                      start=(k == 0), stop=(k == 1)),
                        pe_proj, opt(t_in, t_w, x_free[0]))
            if j == CH // P - 1:
                ctx_used[i] = t
            old = pv_done[(b * NG - 1) * KT + t_] if b else None
            x_free[0] = val_written[b, t_] = put("act", lambda e: e.activation(
                vals[:, t_].rearrange("p (h w) -> p h w", w=VW)[:, :, 0:HD],
                dst.rearrange("p (h w) -> p h w", w=HD), ACT.Copy), act_val, opt(t, old, t_vones))

        def max_task(g, n):
            hq, c = divmod(n, NCH)
            h, qt = divmod(hq, 2)
            i = n_max[0] % 2
            n_max[0] += 1
            dst = bank(M_BANKS[i])
            t = put("pe", lambda e: e.matmul(dst, qstack[g % 3][0:STK, h, qt * P:(qt + 1) * P],
                                             kstack[g % 3][0:STK, h, c * CH:(c + 1) * CH], start=True, stop=True),
                    pe_max, opt(k_ready[g], q_ready[g], max_used[i]) + setup_done)
            max_used[i] = put("dve", lambda e: e.reduce_max(part_max[:, hq, c:c + 1], dst, AX_X), dve_max,
                              opt(t, (dve_neg, dve_neg.value)))

        def max_end(g):
            t = put("dve", lambda e: e.tensor_reduce(neg_max, part_max, AX_X, ALU.max, negate=True), dve_neg,
                    [max_used[0], max_used[1]])
            t = put("dve", lambda e: e.tensor_copy(neg_parts[:, 0], neg_max), dve_neg, [t, (pe_end, pe_end.value)])
            t = put("dve", lambda e: e.tensor_tensor(neg_rest, neg_max, neg_parts[:, 0], ALU.subtract), dve_neg, [t])
            t = put("dve", lambda e: e.tensor_copy(neg_parts[:, 1], neg_rest), dve_neg, [t])
            t = put("dve", lambda e: e.tensor_tensor(neg_parts[:, 2], neg_rest, neg_parts[:, 1], ALU.subtract),
                    dve_neg, [t])
            both = bank(M_BANKS[0], 2)
            for hq in range(GH * 2):
                t2 = put("pe", lambda e, hq=hq: e.matmul(both[STK:ROWS, hq * P:(hq + 1) * P], neg_parts[:, :, hq],
                                                         identb, start=True, stop=True),
                         pe_end, [t, max_used[0], max_used[1], t_identb])
            t = put("dve", lambda e: e.tensor_copy(qstack[g % 3][STK:ROWS].rearrange("p h t -> p (h t)"),
                                                   both[STK:ROWS]), dve_neg, [t2])
            max_used[0] = max_used[1] = neg_ready[g] = t

        def scores(g, t_):
            n = g * KT + t_
            dst = bank(S_BANKS[n % 2], 2)
            w = opt(k_ready[g], neg_ready[g], exp_done[n - 2] if n >= 2 else None, t_ones) + setup_done
            for h in range(GH):
                t = put("pe", lambda e, h=h: e.matmul(dst[:, h * SEQ:(h + 1) * SEQ],
                                                      kstack[g % 3][0:ROWS, h, t_ * P:(t_ + 1) * P],
                                                      qstack[g % 3][0:ROWS, h], start=True, stop=True), pe_score, w)
            scores_done[g] = t
            exp_done.append(put("act", lambda e: e.activation(wts[n % 2], dst, ACT.Exp), act_exp,
                                opt(t, pv_done[n - 2] if n >= 2 else None) + setup_done))

        def weigh(g, t_):
            n = g * KT + t_
            b, hg = divmod(g, NG)
            w = opt(exp_done[n], val_written[b, t_], o_read[0], t_vones)
            for j in range(GH):
                h = hg * GH + j
                t = put("pe", lambda e, j=j, h=h: e.matmul(
                    bank(O_BANK)[32 * j:32 * j + VW, 0:SEQ], vals[:, t_, h * VW:(h + 1) * VW],
                    wts[n % 2][:, j * SEQ:(j + 1) * SEQ], start=(t_ == 0), stop=(t_ == KT - 1)), pe_pv, w)
            pv_done.append(t)

        o_read = [t_zero]
        norm_done = {}

        def end_copy(last):
            o_read[0] = put("dve", lambda e: e.tensor_copy(o_raw, bank(O_BANK)[:, 0:SEQ]), dve_end,
                            opt(last, (pe_end, pe_end.value)))

        def end_norm(hg, bias):
            xb = bank(X_BANK)[:, 0:SEQ]
            t = put("pe", lambda e: e.matmul(xb, lsel, o_raw, start=True, stop=True), pe_end,
                    opt(o_read[0], x_free[0]))
            x_free[0] = t = put("dve", lambda e: e.reciprocal(o_rl, xb), dve_end, [t])
            t = put("dve", lambda e: e.tensor_tensor(o_norm[:, hg], o_raw, o_rl, ALU.mult), dve_end,
                    opt(t, (pe_out, pe_out.value)))
            norm_done[hg] = put("dve", lambda e: e.tensor_scalar_add(o_norm[:, hg], o_norm[:, hg], bias[:, hg:hg + 1]),
                                dve_end, [t])

        pe_out = counter("pe_out")
        x_done = []

        def out_project(b, qt, w):
            xb = bank(X_BANK)[:, 0:EMB]
            for hg in range(NG):
                t = put("pe", lambda e, hg=hg: e.matmul(xb, o_norm[:, hg, qt * P:(qt + 1) * P], w[:, hg],
                                                        start=(hg == 0), stop=(hg == NG - 1)),
                        pe_out, opt(norm_done[NG - 1], x_free[0]))
            i = b * (SEQ // P) + qt
            x_free[0] = put("dve", lambda e: e.tensor_tensor(x[:, i], xb, x[:, i], ALU.add), dve_end, [t])

        def finish_tasks(g):
            b, hg = divmod(g, NG)
            todo = {1: lambda: end_norm(hg, bv)}
            if hg == NG - 1:
                todo[3] = lambda: out_project(b, 0, wo)
                todo[4] = lambda: out_project(b, 1, wo)
            return todo

        MAXES = GH * 2 * NCH
        for s in range(-2, GROUPS + 1):
            nxt = s + 1
            if s % 2 != 0 and s + 2 < GROUPS:
                scatter_k(s + 2)
            if s + 2 < GROUPS:
                load_q(s + 2)
            todo = finish_tasks(s - 1) if s >= 1 else {}
            given = 0
            for t_ in range(KT + 1):
                if 0 <= s < GROUPS and t_ < KT:
                    scores(s, t_)
                if 0 <= nxt < GROUPS:
                    while given < min(MAXES, (t_ + 1) * MAXES // (KT - 4)):
                        max_task(nxt, given)
                        given += 1
                    if t_ == KT - 3:
                        max_end(nxt)
                if t_ > 0 and 0 <= s < GROUPS:
                    weigh(s, t_ - 1)
                if t_ in todo:
                    todo[t_]()
                if s % 2 == 0 and (s + 2) // 2 < GROUPS // 2 and t_ % 2 == 1 and t_ < 2 * NCH:
                    project_k((s + 2) // 2, t_ // 2)
                    if t_ // 2 == NCH - 1:
                        scatter_k(s + 2)
                if s % NG == NG - 1 and (s + 1) // NG < BATCH and t_ > 0:
                    project_v((s + 1) // NG, t_ - 1)
            if 0 <= s < GROUPS:
                end_copy(pv_done[-1])

        fresh = phase_end()
        top[0] = kept
        xn2 = carve((TT, EMB))
        xT2 = carve((KE, TOK))
        wqkv = carve((KE, 3 * EMB))
        wo2 = carve((NG, EMB))
        bqkv = carve((2 * KE,))
        bv2 = carve((NG,))
        bo2 = carve((EMB,))
        wmask = carve((2, WIN))
        hmask = carve((P // HD,))
        q2 = carve((KE, TOK))
        qm = carve((HEADS, TOK))
        k2 = carve((KE, TOK))
        vals2 = carve((TT, HEADS * VW))
        biased = [carve((GH, WIN)) for _ in range(2)]
        nmax = [carve((GH,)) for _ in range(2)]
        wt2 = [carve((GH, WIN)) for _ in range(2)]
        wTa = [carve((GH * P,)) for _ in range(2)]
        wTb = [carve((GH * P,)) for _ in range(2)]

        ld_b = counter("ld_b")
        for dst, src in ((wqkv, "w_qkv"), (wo2, "w_out"), (bqkv, "b_qk"), (bv2, "b_v"), (bo2, "b_out"),
                         (wmask, "wmask"), (hmask, "hmask")):
            t_wb = dma("sp", dst, a[src], ld_b, fresh)
        pool_b = counter("pool_b")
        t_vones = put("pool", lambda e: e.memset(vals2.rearrange("p t (h w) -> p t h w", w=VW)[:, :, :, HD], 1.0),
                      pool_b, fresh)
        t_xT = layernorm_T(xT2, xn2, fresh, (0, 1))
        pe_qkv, dve_qkv = counter("pe_qkv"), counter("dve_qkv")
        for i in range(TT):
            t_bo = put("dve", lambda e, i=i: e.tensor_tensor(x[:, i], x[:, i], bo2, ALU.add), dve_qkv,
                       [t_wb, (dve_ln, dve_ln.value)])
        free = [None, None]
        n = 0
        for m in range(2 * KE):
            for half in range(2):
                dst = bank(2 + n % 2)
                for k in range(KE):
                    t = put("pe", lambda e, m=m, half=half, k=k, dst=dst: e.matmul(
                        dst, wqkv[:, k, m * P:(m + 1) * P], xT2[:, k, half * CH:(half + 1) * CH],
                        start=(k == 0), stop=(k == KE - 1)), pe_qkv, opt(t_xT, t_wb, free[n % 2]))
                to = (q2 if m < KE else k2)[:, m % KE, half * CH:(half + 1) * CH]
                sc = QSCALE if m < KE else 1.0
                free[n % 2] = put("dve", lambda e, m=m, dst=dst, to=to, sc=sc: e.tensor_scalar(
                    to, dst, bqkv[:, m:m + 1], sc, ALU.add, ALU.mult), dve_qkv, [t])
                n += 1
            if m < KE:
                for j in range(P // HD):
                    t_qm = put("dve", lambda e, m=m, j=j: e.tensor_scalar_mul(
                        qm[:, m * (P // HD) + j], q2[:, m], hmask[:, j:j + 1]), dve_qkv, [free[0], free[1]])
        for i in range(TT):
            dst = bank(2 + n % 2)[:, 0:EMB]
            for k in range(KE):
                t = put("pe", lambda e, i=i, k=k, dst=dst: e.matmul(
                    dst, xT2[:, k, i * P:(i + 1) * P], wqkv[:, k, 2 * EMB:3 * EMB],
                    start=(k == 0), stop=(k == KE - 1)), pe_qkv, opt(t_xT, t_wb, free[n % 2]))
            free[n % 2] = put("dve", lambda e, i=i, dst=dst: e.tensor_copy(
                vals2[:, i].rearrange("p (h w) -> p h w", w=VW)[:, :, 0:HD],
                dst.rearrange("p (h w) -> p h w", w=HD)), dve_qkv, [t, t_vones])
            n += 1
        qkv_done = [free[0], free[1], t_qm, t_vones]

        pe_s2, dve_s2, act_s2, pe_t2, act_t2, dve_t2, pe_v2 = (counter(n) for n in (
            "pe_s2", "dve_s2", "act_s2", "pe_t2", "act_t2", "dve_t2", "pe_v2"))
        s_read = [None, None]
        t_read = [None, None]
        w_read = [None, None]
        wT_read = [None, None]
        soft = {}

        def softmax2(u):
            b, hg, qt = u // 8, (u // 2) % 4, u % 2
            i = u % 2
            at = b * SEQ + qt * (SEQ - WIN)
            tok = b * SEQ + qt * P
            dst = bank(2 * i, 2).rearrange("p (h w) -> p h w", h=GH)[:, :, 0:WIN]
            for j in range(GH):
                h = hg * GH + j
                t = put("pe", lambda e, j=j, h=h: e.matmul(
                    dst[:, j], qm[:, h, tok:tok + P], k2[:, h // (P // HD), at:at + WIN], start=True, stop=True),
                    pe_s2, opt(s_read[i]) + qkv_done)
            s_read[i] = t = put("dve", lambda e: e.tensor_tensor(
                biased[i], dst, wmask[:, qt:qt + 1].broadcast_to([P, GH, WIN]), ALU.add), dve_s2, opt(t, w_read[i]))
            t = put("dve", lambda e: e.tensor_reduce(nmax[i], biased[i], AX_X, ALU.max, negate=True), dve_s2, [t])
            for j in range(GH):
                t2 = put("act", lambda e, j=j: e.activation(wt2[i][:, j], biased[i][:, j], ACT.Exp,
                                                            bias=nmax[i][:, j:j + 1]), act_s2, opt(t, w_read[i]))
            soft[u] = t2

        def weigh2(u):
            b, hg, qt = u // 8, (u // 2) % 4, u % 2
            i = u % 2
            full, edge = ((0, P), (P, 0)) if qt == 0 else ((HALF, P), (0, P - HALF))
            ft, et = 2 * b + qt, 2 * b + 1 - qt
            lo = edge[1]
            for j in range(GH):
                put("pe", lambda e, j=j: e.matmul(bank(4)[:, j * P:(j + 1) * P], wt2[i][:, j, full[0]:full[0] + P],
                                                  identf, start=True, stop=True), pe_t2, opt(soft[u], t_read[0]))
            t_a = (pe_t2, pe_t2.value)
            for j in range(GH):
                t = put("pe", lambda e, j=j: e.matmul(bank(5)[lo:lo + HALF, j * P:(j + 1) * P],
                                                      wt2[i][:, j, edge[0]:edge[0] + HALF],
                                                      identf, start=True, stop=True), pe_t2, opt(t_read[1]))
            w_read[i] = t
            t_read[0] = ta = put("act", lambda e: e.activation(wTa[i], bank(4), ACT.Copy), act_t2,
                                 opt(t_a, wT_read[i]))
            t_read[1] = tb = put("dve", lambda e: e.tensor_copy(wTb[i][lo:lo + HALF], bank(5)[lo:lo + HALF]),
                                 dve_t2, opt(t, wT_read[i]))
            o = bank(O_BANK)
            for j in range(GH):
                h = hg * GH + j
                put("pe", lambda e, j=j, h=h: e.matmul(
                    o[32 * j:32 * j + VW, qt * P:(qt + 1) * P], vals2[:, ft, h * VW:(h + 1) * VW],
                    wTa[i][:, j * P:(j + 1) * P], start=True, stop=False), pe_v2, opt(ta, o_read[0]) + qkv_done)
            for j in range(GH):
                h = hg * GH + j
                t = put("pe", lambda e, j=j, h=h: e.matmul(
                    o[32 * j:32 * j + VW, qt * P:(qt + 1) * P], vals2[lo:lo + HALF, et, h * VW:(h + 1) * VW],
                    wTb[i][lo:lo + HALF, j * P:(j + 1) * P], start=False, stop=True,
                    tile_position=(lo, 32 * j)), pe_v2, [tb])
            wT_read[i] = t
            if qt == 1:
                end_copy(t)
                end_norm(hg, bv2)
                if hg == NG - 1:
                    out_project(b, 0, wo2)
                    out_project(b, 1, wo2)

        UNITS = BATCH * NG * 2
        for u in range(UNITS + 1):
            if u < UNITS:
                softmax2(u)
            if u:
                weigh2(u - 1)

        fresh = phase_end()
        top[0] = kept
        xn3 = carve((TT, EMB))
        xT3 = carve((KE, TOK))
        wr = carve((KE, BANKS))
        brb = carve((BANKS,))
        b1 = carve((BANKS, HC))
        b2 = carve((EMB,))
        iota16 = carve((BANKS,))
        lg = carve((TT, BANKS))
        lmax = carve((TT,))
        pr = carve((TT, BANKS))
        psumr = carve((TT,))
        prec = carve((TT,))
        top8 = carve((TT, 8))
        idx8 = carve((TT, 8), U32)
        idxf = carve((TT, 2))
        gate = carve((TT, BANKS))
        gtmp = carve((BANKS,))
        gT = carve((TOK,))
        onerow = carve((BANKS, P))
        gbc = [carve((TOK,)) for _ in range(2)]
        w1s = [carve((KE, HID)) for _ in range(2)]
        w2s = [carve((HC, EMB)) for _ in range(2)]
        NH = 4
        hr = [carve((CH,)) for _ in range(NH)]
        hg_ = [carve((CH,)) for _ in range(NH)]
        outT = carve((KE, TOK))

        ld_c = counter("ld_c")
        for dst, src in ((wr, "Wr"), (brb, "br"), (b1, "b1"), (b2[0:BANKS], "b2"), (iota16, "iota16"),
                         (onerow[0:BANKS], "onerow")):
            t_wc = dma("sp", dst, a[src], ld_c, fresh)
        ld_w1 = [counter(f"ld_w1{i}") for i in range(2)]
        w_used = [None, None]
        w_in = {}

        def load_bank(e_):
            i = e_ % 2
            dma("sp", w1s[i], a["W1"][e_], ld_w1[i], fresh + opt(w_used[i]))
            w_in[e_] = dma("sp", w2s[i], a["W2"][e_], ld_w1[i], fresh + opt(w_used[i]))

        load_bank(0)
        load_bank(1)
        t_xT = layernorm_T(xT3, xn3, fresh, (0, 1))
        pe_r, dve_r, act_r = counter("pe_r"), counter("dve_r"), counter("act_r")
        for i in range(TT):
            for k in range(KE):
                t = put("pe", lambda e, i=i, k=k: e.matmul(bank(2)[:, i * BANKS:(i + 1) * BANKS],
                                                           xT3[:, k, i * P:(i + 1) * P], wr[:, k],
                                                           start=(k == 0), stop=(k == KE - 1)), pe_r, [t_xT, t_wc])
        lgp = bank(2)[:, 0:TT * BANKS].rearrange("p (t e) -> p t e", t=TT)
        t = put("dve", lambda e: e.tensor_tensor(
            lg, lgp, brb.rearrange("p (o e) -> p o e", o=1).broadcast_to([P, TT, BANKS]), ALU.add), dve_r, [t])
        t = put("dve", lambda e: e.reduce_max(lmax, lg, AX_X), dve_r, [t])
        t = put("dve", lambda e: e.tensor_tensor(
            lg, lg, lmax.rearrange("p (t o) -> p t o", o=1).broadcast_to([P, TT, BANKS]), ALU.subtract), dve_r, [t])
        t = put("act", lambda e: e.activation(pr, lg, ACT.Exp), act_r, [t])
        t = put("dve", lambda e: e.reduce_sum(psumr, pr, AX_X), dve_r, [t])
        t = put("dve", lambda e: e.reciprocal(prec, psumr), dve_r, [t])
        t = put("dve", lambda e: e.tensor_tensor(
            pr, pr, prec.rearrange("p (t o) -> p t o", o=1).broadcast_to([P, TT, BANKS]), ALU.mult), dve_r, [t])
        for i in range(TT):
            t2 = put("dve", lambda e, i=i: e.max(top8[:, i], pr[:, i]), dve_r, [t])
            t2 = put("dve", lambda e, i=i: e.max_index(idx8[:, i], top8[:, i], pr[:, i]), dve_r, [t2])
        t = put("dve", lambda e: e.tensor_copy(idxf, idx8[:, :, 0:2]), dve_r, [t2])
        for i in range(TT):
            t = put("dve", lambda e, i=i: e.tensor_scalar(gate[:, i], iota16, idxf[:, i, 0:1], top8[:, i, 0:1],
                                                          ALU.is_equal, ALU.mult), dve_r, [t, t_wc])
            t = put("dve", lambda e, i=i: e.tensor_scalar(gtmp, iota16, idxf[:, i, 1:2], top8[:, i, 1:2],
                                                          ALU.is_equal, ALU.mult), dve_r, [t])
            t = put("dve", lambda e, i=i: e.tensor_tensor(gate[:, i], gate[:, i], gtmp, ALU.add), dve_r, [t])
        for i in range(TT):
            t2 = put("pe", lambda e, i=i: e.matmul(bank(i // 4)[0:BANKS, (i % 4) * P:(i % 4 + 1) * P], gate[:, i],
                                                   identf, start=True, stop=True), pe_r, [t, (act_lnT, act_lnT.value)])
        t_gT = put("dve", lambda e: e.tensor_copy(gT[0:BANKS], bank(0, 2)[0:BANKS]), dve_r, [t2])

        pe_h, act_h, dve_h, pe_y, pe_g, act_g = (counter(n) for n in ("pe_h", "act_h", "dve_h", "pe_y", "pe_g", "act_g"))
        for m in range(KE):
            for half in range(2):
                put("pe", lambda e, m=m, half=half: e.matmul(
                    bank(4 + 2 * m + half), b2[0:BANKS, m * P:(m + 1) * P],
                    gT[0:BANKS, half * CH:(half + 1) * CH], start=True, stop=False), pe_y, [t_gT, t_wc])
        h_read = [t_gT] * NH
        hg_read = [None] * NH
        gb_done = {}
        gb_used = [None, None]
        jobs = [(e_, hc, half) for e_ in range(BANKS) for hc in range(HC) for half in range(2)]

        nb = [0]

        def up(n):
            e_, hc, half = jobs[n]
            if hc == 0 and half == 0:
                for hf in range(2):
                    i = nb[0] % NH
                    nb[0] += 1
                    t = put("pe", lambda e, i=i, hf=hf, e_=e_: e.matmul(
                        bank(i), onerow[0:BANKS, e_], gT[0:BANKS, hf * CH:(hf + 1) * CH], start=True, stop=True),
                        pe_g, [h_read[i], t_gT])
                    h_read[i] = put("act", lambda e, i=i, hf=hf, e_=e_: e.activation(
                        gbc[e_ % 2][:, hf * CH:(hf + 1) * CH], bank(i), ACT.Copy), act_g, opt(t, gb_used[e_ % 2]))
                gb_done[e_] = h_read[i]
            i = nb[0] % NH
            nb[0] += 1
            for k in range(KE):
                t = put("pe", lambda e, k=k, i=i: e.matmul(
                    bank(i), w1s[e_ % 2][:, k, hc * P:(hc + 1) * P], xT3[:, k, half * CH:(half + 1) * CH],
                    start=(k == 0), stop=(k == KE - 1)), pe_h, [w_in[e_], h_read[i]])
            s = n % NH
            h_read[i] = t = put("act", lambda e, i=i: e.activation(hr[s], bank(i), ACT.Relu,
                                                                   bias=b1[:, e_, hc:hc + 1]),
                                act_h, opt(t, (dve_h, dve_h.value - NH + 1) if dve_h.value >= NH else None))
            up_done[n] = put("dve", lambda e: e.tensor_tensor(hg_[s], hr[s], gbc[e_ % 2][:, half * CH:(half + 1) * CH],
                                                              ALU.mult), dve_h, opt(t, gb_done[e_], hg_read[s]))
            gb_used[e_ % 2] = up_done[n]

        up_done = {}

        def down(n):
            e_, hc, half = jobs[n]
            s = n % NH
            for m in range(KE):
                t = put("pe", lambda e, m=m: e.matmul(
                    bank(4 + 2 * m + half), w2s[e_ % 2][:, hc, m * P:(m + 1) * P], hg_[s],
                    start=False, stop=(e_ == BANKS - 1 and hc == HC - 1)), pe_y, [up_done[n]])
            hg_read[s] = t
            if hc == HC - 1 and half == 1:
                w_used[e_ % 2] = t
                if e_ + 2 < BANKS:
                    load_bank(e_ + 2)

        LAG = 2
        for n in range(len(jobs) + LAG):
            if n < len(jobs):
                up(n)
            if n >= LAG:
                down(n - LAG)

        act_o, pe_o, dve_o, st_o = counter("act_o"), counter("pe_o"), counter("dve_o"), counter("st_o")
        for m in range(KE):
            t_o = put("act", lambda e, m=m: e.activation(outT[:, m], bank(4 + 2 * m, 2), ACT.Copy), act_o,
                      [(pe_y, pe_y.value)])
        o_free = [h_read[0], h_read[1], h_read[2], h_read[3]]
        for i in range(TT):
            dst = bank(i % 4)[:, 0:EMB]
            for m in range(KE):
                t = put("pe", lambda e, i=i, m=m, dst=dst: e.matmul(
                    dst[:, m * P:(m + 1) * P], outT[:, m, i * P:(i + 1) * P], identf, start=True, stop=True),
                    pe_o, [t_o, o_free[i % 4]])
            o_free[i % 4] = t = put("dve", lambda e, i=i, dst=dst: e.tensor_tensor(x[:, i], dst, x[:, i], ALU.add),
                                    dve_o, [t])
            dma("sp", out[:, i], x[:, i], st_o, [t])
        put("sp", None, None, [(st_o, st_o.value)])

        block = ctx.enter_context(nc.Block())

        def play(name, e):
            for waits, make, sem, by in queue[name]:
                for s, v in waits:
                    e.wait_ge(s, v)
                if make is not None:
                    i = make(e)
                    if sem is not None:
                        i.then_inc(sem, by)

        @block.tensor
        def _(e):
            play("pe", e)

        @block.scalar
        def _(e):
            play("act", e)

        @block.vector
        def _(e):
            play("dve", e)

        @block.gpsimd
        def _(e):
            play("pool", e)

        @block.sync
        def _(e):
            play("sp", e)


def layouts(i):
    f = np.float32

    def rows(w, k, p=P):
        return np.ascontiguousarray(w.reshape(k, p, -1).transpose(1, 0, 2))

    def by_head(w):
        w = w.reshape(NG, GH, HD, -1)
        o = np.zeros((NG, GH, 32, w.shape[-1]), f)
        o[:, :, :HD] = w
        return np.ascontiguousarray(o.reshape(NG, P, -1).transpose(1, 0, 2))

    def spread(v):
        return np.ascontiguousarray(np.broadcast_to(v, (P,) + v.shape))

    q = np.arange(P)[:, None, None]
    j = np.arange(WIN)[None, None, :]
    t = np.arange(2)[None, :, None]
    dist = np.abs(P * t + q - ((SEQ - WIN) * t + j))
    p = np.arange(P)
    bqkv = i["L0_attn_b_qkv"]
    return {
        "x": rows(i["x"].reshape(TOK, EMB), TT),
        "ctxT": np.ascontiguousarray(i["ctx_768"].reshape(BATCH, KV, 2, KC).transpose(0, 3, 2, 1)),
        "wqT": rows(i["L0_xattn_wq"].T, KE),
        "wkT": rows(i["L0_xattn_wk"].T, 2, KC),
        "wvT": rows(i["L0_xattn_wv"].T, 2, KC),
        "woT": by_head(i["L0_xattn_wo"].T),
        "bq": np.ascontiguousarray(i["L0_xattn_bq"].reshape(KE, P).T),
        "bk": np.ascontiguousarray(i["L0_xattn_bk"].reshape(KE, P).T),
        "bv": by_head(i["L0_xattn_bv"])[:, :, 0].copy(),
        "bo": spread(i["L0_xattn_bo"]),
        "w_qkv": rows(i["L0_attn_w_qkv"], KE),
        "w_out": by_head(i["L0_attn_w_out"]),
        "b_qk": np.ascontiguousarray(bqkv[:2 * EMB].reshape(2 * KE, P).T),
        "b_v": by_head(bqkv[2 * EMB:])[:, :, 0].copy(),
        "b_out": spread(i["L0_attn_b_out"]),
        "Wr": rows(i["L0_ffn_Wr"], KE),
        "br": spread(i["L0_ffn_br"]),
        "W1": np.ascontiguousarray(i["L0_ffn_W1"].reshape(BANKS, KE, P, HID).transpose(0, 2, 1, 3)),
        "b1": np.ascontiguousarray(i["L0_ffn_b1"].reshape(BANKS, HC, P).transpose(2, 0, 1)),
        "W2": np.ascontiguousarray(i["L0_ffn_W2"].reshape(BANKS, HC, P, EMB).transpose(0, 2, 1, 3)),
        "b2": i["L0_ffn_b2"],
        "identf": np.eye(P, dtype=f),
        "lsel": (p[:, None] == (p[None, :] // 32) * 32 + HD).astype(f),
        "wmask": np.where(dist <= HALF, f(0), f(-3e38)).astype(f),
        "hmask": (p[:, None] // HD == np.arange(P // HD)[None, :]).astype(f),
        "iota16": spread(np.arange(BANKS, dtype=f)),
        "onerow": np.repeat(np.eye(BANKS, dtype=f)[:, :, None], P, axis=2),
    }


def kernel(**inputs):
    import concourse.bacc as bacc
    from concourse.bass_utils import run_bass_kernel_spmd

    nc = bacc.Bacc("TRN2", target_bir_lowering=False, num_devices=1)
    arrays, aps = {}, {}
    for name, v in layouts({k: np.asarray(v) for k, v in inputs.items()}).items():
        arrays[f"in_{name}"] = v
        aps[name] = nc.dram_tensor(f"in_{name}", v.shape, mybir.dt.from_np(v.dtype), kind="ExternalInput").ap()
    out = nc.dram_tensor("out", (P, TT, EMB), F32, kind="ExternalOutput").ap()
    scratch = {"qparts": nc.dram_tensor("qparts", (3, EMB, TOK), BF16, kind="Internal").ap()}
    build(nc, aps, out, scratch)
    r = run_bass_kernel_spmd(nc, [arrays], core_ids=[0])
    return np.ascontiguousarray(r.results[0]["out"].transpose(1, 0, 2)).reshape(BATCH, SEQ, EMB)
```

```python
from contextlib import ExitStack

import numpy as np

import concourse.bass as bass
from concourse import mybir

F32 = mybir.dt.float32
BF16 = mybir.dt.bfloat16
U32 = mybir.dt.uint32
I32 = mybir.dt.int32
ACT = mybir.ActivationFunctionType
ALU = mybir.AluOpType
AX_X = mybir.AxisListType.X

P = 128
BATCH, SEQ, EMB = 4, 256, 256
KV, CTX = 4096, 192
HEADS, HD = 16, 16
TOK = BATCH * SEQ
TT = TOK // P
KE = EMB // P
KC = CTX // 2
GH = 4
GROUPS = BATCH * HEADS // GH
NG = HEADS // GH
KT = KV // P
CH = 512
NCH = KV // CH
VW = HD + 1
SLOTS = 6
K_PART = (0, 0, 0, 1, 1, 2)
Q_PART = (0, 1, 2, 0, 1, 0)
STK = SLOTS * HD
ROWS = STK + 3
QSCALE = 1.0 / HD ** 0.5
EPS = 1e-5
HALF = 32
WIN = P + HALF
BANKS, HID, NSEL = 16, 1024, 2
HC = HID // P
SLOT_TILES = NSEL * TOK // P + BANKS - 1


class Counter:

    def __init__(self, sem):
        self.sem, self.value = sem, 0


def build(nc, a, out, scratch):
    ctx = ExitStack()
    with ctx:
        def counter(name):
            return Counter(ctx.enter_context(nc.semaphore(name)))

        queue = {n: [] for n in ("pe", "act", "dve", "pool", "sp")}
        waited = {n: {} for n in queue}
        every = []

        def put(engine, make, sem, after=(), by=1):
            waits = []
            for c, v in after:
                if waited[engine].get(c, 0) < v:
                    waited[engine][c] = v
                    waits.append((c.sem, v))
            if sem is not None:
                sem.value += by
                if sem not in every:
                    every.append(sem)
            queue[engine].append((waits, make, sem.sem if sem else None, by))
            return (sem, sem.value) if sem else None

        def dma(engine, dst, src, sem, after=()):
            return put(engine, lambda e, d=dst, s=src: e.dma_start(d, s), sem, after, 16)

        def phase_end():
            return [(c, c.value) for c in every]

        arena = ctx.enter_context(nc.sbuf_tensor("arena", [P, 52600], F32))
        top = [0]

        def carve(shape, dt=F32):
            n = int(np.prod(shape)) * (2 if dt == BF16 else 4)
            n = (n + 3) // 4
            v = arena[:, top[0]:top[0] + n]
            top[0] += n
            assert top[0] <= 52600, top[0]
            if dt != F32:
                v = v.bitcast(dt)
            if len(shape) == 2:
                v = v.rearrange("p (a b) -> p a b", a=shape[0])
            elif len(shape) == 3:
                v = v.rearrange("p (a b c) -> p a b c", a=shape[0], b=shape[1])
            return v

        psum = ctx.enter_context(nc.psum_tensor("psum", [P, 8 * 512], F32))

        def bank(i, n=1):
            return psum[:, i * 512:(i + n) * 512]

        x = carve((TT, EMB))
        identf = carve((P,))
        identb = carve((P,), BF16)
        lsel = carve((P,))
        stats = carve((TT, 6))
        mv = carve((TT, 2))
        rstd = carve((TT,))
        rtmp = carve((2, TT))
        o_raw = carve((SEQ,))
        o_rl = carve((SEQ,))
        o_norm = carve((NG, SEQ))
        kept = top[0]

        ld_const = counter("ld_const")
        dve_ln = counter("dve_ln")
        pe_lnT = counter("pe_lnT")
        act_lnT = counter("act_lnT")
        act_ln = counter("act_ln")

        dma("sp", x, a["x"], ld_const)
        for dst, src in ((identf, "identf"), (lsel, "lsel")):
            t_const = dma("sp", dst, a[src], ld_const)
        t_identb = put("dve", lambda e: e.tensor_copy(identb, identf), dve_ln, [t_const])

        def layernorm_T(xT, xn, after, banks):
            for i in range(TT):
                put("dve", lambda e, i=i: e.bn_stats(stats[:, i, :], x[:, i, :]), dve_ln, after)
            t = (dve_ln, dve_ln.value)
            for i in range(TT):
                t2 = put("dve", lambda e, i=i: e.bn_aggr(mv[:, i, :], stats[:, i, :]), dve_ln, [t])
            var = rtmp[:, 0, :]
            t = put("dve", lambda e: e.tensor_scalar_add(var, mv[:, :, 1], EPS), dve_ln, [t2])
            t = put("act", lambda e: e.activation(rstd, var, ACT.Ln), act_ln, [t])
            t = put("act", lambda e: e.activation(rstd, rstd, ACT.Exp, scale=-0.5), act_ln, [t])
            sq = rtmp[:, 1, :]
            for _ in range(2):
                t = put("dve", lambda e: e.tensor_tensor(sq, rstd, rstd, ALU.mult), dve_ln, [t])
                t = put("dve", lambda e: e.tensor_tensor(sq, sq, var, ALU.mult), dve_ln, [t])
                t = put("dve", lambda e: e.tensor_scalar(sq, sq, -0.5, 1.5, ALU.mult, ALU.add), dve_ln, [t])
                t = put("dve", lambda e: e.tensor_tensor(rstd, rstd, sq, ALU.mult), dve_ln, [t])
            norm = []
            for i in range(TT):
                norm.append(put("dve", lambda e, i=i: e.tensor_scalar(
                    xn[:, i, :], x[:, i, :], mv[:, i, 0:1], rstd[:, i:i + 1], ALU.subtract, ALU.mult), dve_ln, [t]))
            done, n = [], 0
            evac = [None] * 2
            for k in range(KE):
                for half in range(TT // 4):
                    dst = bank(banks[n % 2])
                    for j in range(4):
                        i = 4 * half + j
                        w = [norm[i], t_const] + ([evac[n % 2]] if evac[n % 2] else [])
                        t = put("pe", lambda e, i=i, j=j, k=k, dst=dst: e.matmul(
                            dst[:, j * P:(j + 1) * P], xn[:, i, k * P:(k + 1) * P], identf, start=True, stop=True),
                            pe_lnT, w)
                    evac[n % 2] = put("act", lambda e, k=k, half=half, dst=dst: e.activation(
                        xT[:, k, half * CH:(half + 1) * CH], dst, ACT.Copy), act_lnT, [t])
                    done.append(evac[n % 2])
                    n += 1
            return done[-1]

        kstack = [carve((GH, KV), BF16) for _ in range(3)]
        setup_at = top[0]
        pieces = carve((3, KV), BF16)
        vals = carve((KT, HEADS * VW))
        ctx_in = [carve((2, CH)) for _ in range(2)]
        wts = [carve((GH * SEQ,)) for _ in range(2)]
        qstack = [carve((GH, SEQ), BF16) for _ in range(3)]
        rest = [carve((CH,)) for _ in range(2)]
        wk = carve((2, EMB))
        wv = carve((2, EMB))
        wo = carve((NG, EMB))
        bk = carve((KE,))
        bv = carve((NG,))
        bq = carve((KE,))
        part_max = carve((GH * 2, NCH))
        neg_max = carve((GH * 2,))
        neg_rest = carve((GH * 2,))
        neg_parts = carve((3, GH * 2), BF16)
        keep_top, top[0] = top[0], setup_at
        xn1 = carve((TT, EMB))
        xT1 = carve((KE, TOK))
        wq = carve((KE, EMB))
        qf = carve((KE, TOK))
        bo_bc = carve((EMB,))
        qparts = carve((3, KE, TOK), BF16)
        qrest = carve((CH,))
        blank = carve((EMB,))
        assert top[0] <= keep_top
        top[0] = keep_top

        ld_w = counter("ld_w")
        dma("sp", wq, a["wqT"], ld_w)
        for dst, src in ((wk, "wkT"), (wv, "wvT")):
            dma("sp", dst[0:KC], a[src], ld_w)
        for dst, src in ((wo, "woT"), (bk, "bk"), (bv, "bv"), (bq, "bq"), (bo_bc, "bo")):
            t_w = dma("sp", dst, a[src], ld_w)

        pool_set = counter("pool_set")
        for s in range(3):
            t_ones = put("pool", lambda e, s=s: e.memset(kstack[s][STK:ROWS], 1.0), pool_set)
        dve_set = counter("dve_set")
        t_zero = put("dve", lambda e: e.memset(psum[:, :], 0.0), dve_set)

        t_blank0 = put("pool", lambda e: e.memset(blank, 0.0), pool_set, [t_ones])
        st_blank = counter("st_blank")
        for j in range(SLOT_TILES):
            t_blank = dma("sp", scratch["slots_x"][j * P:(j + 1) * P], blank, st_blank, [t_blank0])

        t_xT = layernorm_T(xT1, xn1, [t_const, t_zero], (0, 1))
        pe_q, dve_q, act_q, st_q = counter("pe_q"), counter("dve_q"), counter("act_q"), counter("st_q")
        free = [None, None]
        for m in range(KE):
            for half in range(2):
                n = 2 * m + half
                dst = bank(2 + n % 2)
                for k in range(KE):
                    t = put("pe", lambda e, m=m, half=half, k=k, dst=dst: e.matmul(
                        dst, wq[:, k, m * P:(m + 1) * P], xT1[:, k, half * CH:(half + 1) * CH],
                        start=(k == 0), stop=(k == KE - 1)), pe_q, [t_xT, t_w] + [f for f in [free[n % 2]] if f])
                sl = slice(half * CH, (half + 1) * CH)
                free[n % 2] = t = put("dve", lambda e, m=m, sl=sl, dst=dst: e.tensor_scalar(
                    qf[:, m, sl], dst, bq[:, m:m + 1], QSCALE, ALU.add, ALU.mult), dve_q, [t])
                t = put("dve", lambda e, m=m, sl=sl: e.tensor_copy(qparts[:, 0, m, sl], qf[:, m, sl]), dve_q, [t])
                t = put("dve", lambda e, m=m, sl=sl: e.tensor_tensor(
                    qrest, qf[:, m, sl], qparts[:, 0, m, sl], ALU.subtract), dve_q, [t])
                t = put("dve", lambda e, m=m, sl=sl: e.tensor_copy(qparts[:, 1, m, sl], qrest), dve_q, [t])
                t = put("dve", lambda e, m=m, sl=sl: e.tensor_tensor(
                    qparts[:, 2, m, sl], qrest, qparts[:, 1, m, sl], ALU.subtract), dve_q, [t])
        qd = scratch["qparts"].rearrange("s (k p) t -> s p k t", p=P)
        for s in range(3):
            t_qd = dma("sp", qd[s], qparts[:, s], st_q, [t])
        for i in range(TT):
            t_bo = put("dve", lambda e, i=i: e.tensor_tensor(x[:, i, :], x[:, i, :], bo_bc, ALU.add), dve_q,
                       [t_w, (dve_ln, dve_ln.value)])
        setup_done = phase_end()

        t_vones = put("pool", lambda e: e.memset(vals.rearrange("p t (h w) -> p t h w", w=VW)[:, :, :, HD], 1.0),
                      pool_set, setup_done)

        S_BANKS = (0, 2)
        M_BANKS = (4, 5)
        X_BANK, O_BANK = 6, 7

        pe_proj, pe_score, pe_max, pe_pv, pe_end = (counter(n) for n in ("pe_proj", "pe_score", "pe_max", "pe_pv", "pe_end"))
        act_hi, act_exp, act_val = counter("act_hi"), counter("act_exp"), counter("act_val")
        dve_rest, dve_max, dve_end, dve_neg = (counter(n) for n in ("dve_rest", "dve_max", "dve_end", "dve_neg"))
        pool_part = counter("pool_part")
        ld_ctx = [counter(f"ld_ctx{i}") for i in range(2)]
        ld_k = [counter(f"ld_k{i}") for i in range(3)]
        ld_q = [counter(f"ld_q{i}") for i in range(3)]

        x_free = [None]
        ctx_used = [None, None]
        n_ctx = [0]
        ctx_now = [None]
        scores_done = {}
        exp_done = []
        pv_done = []
        max_used = [None, None]
        n_max = [0]
        pieces_read = [[]]
        pieces_ready = {}
        val_written = {}
        k_ready, q_ready, neg_ready = {}, {}, {}

        def opt(*t):
            return [v for v in t if v]

        def load_ctx(b, c):
            i = n_ctx[0] % 2
            n_ctx[0] += 1
            t = dma("sp", ctx_in[i][0:KC], a["ctxT"][b, :, :, c * CH:(c + 1) * CH], ld_ctx[i],
                    opt(ctx_used[i]) + setup_done)
            return i, t

        def load_q(g):
            b, hg = divmod(g, NG)
            after = opt(scores_done.get(g - 3)) + setup_done + [t_qd]
            for s in range(SLOTS):
                src = scratch["qparts"][Q_PART[s], hg * GH * HD:(hg + 1) * GH * HD, b * SEQ:(b + 1) * SEQ]
                t = dma("sp", qstack[g % 3][s * HD:(s + 1) * HD], src.rearrange("(h d) t -> d h t", d=HD),
                        ld_q[g % 3], after)
            q_ready[g] = t

        def scatter_k(g):
            after = opt(scores_done.get(g - 3), *pieces_ready[g // 2])
            for h in range(GH):
                row = ((g % 2) * GH + h) * HD
                for s in range(SLOTS):
                    t = dma("sp", kstack[g % 3][s * HD:(s + 1) * HD, h], pieces[row:row + HD, K_PART[s]],
                            ld_k[g % 3], after)
            k_ready[g] = t
            pieces_read[0] = opt(*pieces_read[0]) + [t]

        def project_k(mt, c):
            b, m = divmod(mt, 2)
            i, t_in = load_ctx(b, c)
            dst = bank(X_BANK)
            for k in range(2):
                t = put("pe", lambda e, k=k: e.matmul(dst, wk[0:KC, k, m * P:(m + 1) * P], ctx_in[i][0:KC, k],
                                                      start=(k == 0), stop=(k == 1)),
                        pe_proj, opt(t_in, t_w, x_free[0]))
            ctx_used[i] = t
            sl = slice(c * CH, (c + 1) * CH)
            hi = pieces[:, 0, sl]
            t_hi = put("act", lambda e: e.activation(hi, dst, ACT.Identity, bias=bk[:, m:m + 1]), act_hi,
                       [t] + pieces_read[0])
            r = rest[c % 2]
            t_r = put("dve", lambda e: e.scalar_tensor_tensor(r, dst, bk[:, m:m + 1], hi, ALU.add, ALU.subtract),
                      dve_rest, opt(t_hi, rest_used[c % 2]))
            x_free[0] = t_r
            t = put("pool", lambda e: e.tensor_copy(pieces[:, 1, sl], r), pool_part, [t_r] + pieces_read[0])
            t = put("pool", lambda e: e.tensor_tensor(pieces[:, 2, sl], r, pieces[:, 1, sl], ALU.subtract),
                    pool_part, [t])
            rest_used[c % 2] = t
            pieces_ready[mt] = [t_hi, t]

        rest_used = [None, None]

        def project_v(b, t_):
            c, j = divmod(t_, CH // P)
            if j == 0:
                ctx_now[0] = load_ctx(b, c)
            i, t_in = ctx_now[0]
            dst = bank(X_BANK)[:, 0:EMB]
            for k in range(2):
                t = put("pe", lambda e, k=k: e.matmul(dst, ctx_in[i][0:KC, k, j * P:(j + 1) * P], wv[0:KC, k],
                                                      start=(k == 0), stop=(k == 1)),
                        pe_proj, opt(t_in, t_w, x_free[0]))
            if j == CH // P - 1:
                ctx_used[i] = t
            old = pv_done[(b * NG - 1) * KT + t_] if b else None
            x_free[0] = val_written[b, t_] = put("act", lambda e: e.activation(
                vals[:, t_].rearrange("p (h w) -> p h w", w=VW)[:, :, 0:HD],
                dst.rearrange("p (h w) -> p h w", w=HD), ACT.Copy), act_val, opt(t, old, t_vones))

        def max_task(g, n):
            hq, c = divmod(n, NCH)
            h, qt = divmod(hq, 2)
            i = n_max[0] % 2
            n_max[0] += 1
            dst = bank(M_BANKS[i])
            t = put("pe", lambda e: e.matmul(dst, qstack[g % 3][0:STK, h, qt * P:(qt + 1) * P],
                                             kstack[g % 3][0:STK, h, c * CH:(c + 1) * CH], start=True, stop=True),
                    pe_max, opt(k_ready[g], q_ready[g], max_used[i]) + setup_done)
            max_used[i] = put("dve", lambda e: e.reduce_max(part_max[:, hq, c:c + 1], dst, AX_X), dve_max,
                              opt(t, (dve_neg, dve_neg.value)))

        def max_end(g):
            t = put("dve", lambda e: e.tensor_reduce(neg_max, part_max, AX_X, ALU.max, negate=True), dve_neg,
                    [max_used[0], max_used[1]])
            t = put("dve", lambda e: e.tensor_copy(neg_parts[:, 0], neg_max), dve_neg, [t, (pe_end, pe_end.value)])
            t = put("dve", lambda e: e.tensor_tensor(neg_rest, neg_max, neg_parts[:, 0], ALU.subtract), dve_neg, [t])
            t = put("dve", lambda e: e.tensor_copy(neg_parts[:, 1], neg_rest), dve_neg, [t])
            t = put("dve", lambda e: e.tensor_tensor(neg_parts[:, 2], neg_rest, neg_parts[:, 1], ALU.subtract),
                    dve_neg, [t])
            both = bank(M_BANKS[0], 2)
            for hq in range(GH * 2):
                t2 = put("pe", lambda e, hq=hq: e.matmul(both[STK:ROWS, hq * P:(hq + 1) * P], neg_parts[:, :, hq],
                                                         identb, start=True, stop=True),
                         pe_end, [t, max_used[0], max_used[1], t_identb])
            t = put("dve", lambda e: e.tensor_copy(qstack[g % 3][STK:ROWS].rearrange("p h t -> p (h t)"),
                                                   both[STK:ROWS]), dve_neg, [t2])
            max_used[0] = max_used[1] = neg_ready[g] = t

        def scores(g, t_):
            n = g * KT + t_
            dst = bank(S_BANKS[n % 2], 2)
            w = opt(k_ready[g], neg_ready[g], exp_done[n - 2] if n >= 2 else None, t_ones) + setup_done
            for h in range(GH):
                t = put("pe", lambda e, h=h: e.matmul(dst[:, h * SEQ:(h + 1) * SEQ],
                                                      kstack[g % 3][0:ROWS, h, t_ * P:(t_ + 1) * P],
                                                      qstack[g % 3][0:ROWS, h], start=True, stop=True), pe_score, w)
            scores_done[g] = t
            exp_done.append(put("act", lambda e: e.activation(wts[n % 2], dst, ACT.Exp), act_exp,
                                opt(t, pv_done[n - 2] if n >= 2 else None) + setup_done))

        def weigh(g, t_):
            n = g * KT + t_
            b, hg = divmod(g, NG)
            w = opt(exp_done[n], val_written[b, t_], o_read[0], t_vones)
            for j in range(GH):
                h = hg * GH + j
                t = put("pe", lambda e, j=j, h=h: e.matmul(
                    bank(O_BANK)[32 * j:32 * j + VW, 0:SEQ], vals[:, t_, h * VW:(h + 1) * VW],
                    wts[n % 2][:, j * SEQ:(j + 1) * SEQ], start=(t_ == 0), stop=(t_ == KT - 1)), pe_pv, w)
            pv_done.append(t)

        o_read = [t_zero]
        norm_done = {}

        def end_copy(last):
            o_read[0] = put("dve", lambda e: e.tensor_copy(o_raw, bank(O_BANK)[:, 0:SEQ]), dve_end,
                            opt(last, (pe_end, pe_end.value)))

        def end_norm(hg, bias):
            xb = bank(X_BANK)[:, 0:SEQ]
            t = put("pe", lambda e: e.matmul(xb, lsel, o_raw, start=True, stop=True), pe_end,
                    opt(o_read[0], x_free[0]))
            x_free[0] = t = put("dve", lambda e: e.reciprocal(o_rl, xb), dve_end, [t])
            t = put("dve", lambda e: e.tensor_tensor(o_norm[:, hg], o_raw, o_rl, ALU.mult), dve_end,
                    opt(t, (pe_out, pe_out.value)))
            norm_done[hg] = put("dve", lambda e: e.tensor_scalar_add(o_norm[:, hg], o_norm[:, hg], bias[:, hg:hg + 1]),
                                dve_end, [t])

        pe_out = counter("pe_out")
        x_done = []

        def out_project(b, qt, w):
            xb = bank(X_BANK)[:, 0:EMB]
            for hg in range(NG):
                t = put("pe", lambda e, hg=hg: e.matmul(xb, o_norm[:, hg, qt * P:(qt + 1) * P], w[:, hg],
                                                        start=(hg == 0), stop=(hg == NG - 1)),
                        pe_out, opt(norm_done[NG - 1], x_free[0]))
            i = b * (SEQ // P) + qt
            x_free[0] = put("dve", lambda e: e.tensor_tensor(x[:, i], xb, x[:, i], ALU.add), dve_end, [t])

        def finish_tasks(g):
            b, hg = divmod(g, NG)
            todo = {1: lambda: end_norm(hg, bv)}
            if hg == NG - 1:
                todo[3] = lambda: out_project(b, 0, wo)
                todo[4] = lambda: out_project(b, 1, wo)
            return todo

        MAXES = GH * 2 * NCH
        for s in range(-2, GROUPS + 1):
            nxt = s + 1
            if s % 2 != 0 and s + 2 < GROUPS:
                scatter_k(s + 2)
            if s + 2 < GROUPS:
                load_q(s + 2)
            todo = finish_tasks(s - 1) if s >= 1 else {}
            given = 0
            for t_ in range(KT + 1):
                if 0 <= s < GROUPS and t_ < KT:
                    scores(s, t_)
                if 0 <= nxt < GROUPS:
                    while given < min(MAXES, (t_ + 1) * MAXES // (KT - 4)):
                        max_task(nxt, given)
                        given += 1
                    if t_ == KT - 3:
                        max_end(nxt)
                if t_ > 0 and 0 <= s < GROUPS:
                    weigh(s, t_ - 1)
                if t_ in todo:
                    todo[t_]()
                if s % 2 == 0 and (s + 2) // 2 < GROUPS // 2 and t_ % 2 == 1 and t_ < 2 * NCH:
                    project_k((s + 2) // 2, t_ // 2)
                    if t_ // 2 == NCH - 1:
                        scatter_k(s + 2)
                if s % NG == NG - 1 and (s + 1) // NG < BATCH and t_ > 0:
                    project_v((s + 1) // NG, t_ - 1)
            if 0 <= s < GROUPS:
                end_copy(pv_done[-1])

        fresh = phase_end()
        top[0] = kept
        xn2 = carve((TT, EMB))
        xT2 = carve((KE, TOK))
        wqkv = carve((KE, 3 * EMB))
        wo2 = carve((NG, EMB))
        bqkv = carve((2 * KE,))
        bv2 = carve((NG,))
        bo2 = carve((EMB,))
        wmask = carve((2, WIN))
        hmask = carve((P // HD,))
        q2 = carve((KE, TOK))
        qm = carve((HEADS, TOK))
        k2 = carve((KE, TOK))
        vals2 = carve((TT, HEADS * VW))
        biased = [carve((GH, WIN)) for _ in range(2)]
        nmax = [carve((GH,)) for _ in range(2)]
        wt2 = [carve((GH, WIN)) for _ in range(2)]
        wTa = [carve((GH * P,)) for _ in range(2)]
        wTb = [carve((GH * P,)) for _ in range(2)]

        ld_b = counter("ld_b")
        for dst, src in ((wqkv, "w_qkv"), (wo2, "w_out"), (bqkv, "b_qk"), (bv2, "b_v"), (bo2, "b_out"),
                         (wmask, "wmask"), (hmask, "hmask")):
            t_wb = dma("sp", dst, a[src], ld_b, fresh)
        pool_b = counter("pool_b")
        t_vones = put("pool", lambda e: e.memset(vals2.rearrange("p t (h w) -> p t h w", w=VW)[:, :, :, HD], 1.0),
                      pool_b, fresh)
        t_xT = layernorm_T(xT2, xn2, fresh, (0, 1))
        pe_qkv, dve_qkv = counter("pe_qkv"), counter("dve_qkv")
        for i in range(TT):
            t_bo = put("dve", lambda e, i=i: e.tensor_tensor(x[:, i], x[:, i], bo2, ALU.add), dve_qkv,
                       [t_wb, (dve_ln, dve_ln.value)])
        free = [None, None]
        n = 0
        for m in range(2 * KE):
            for half in range(2):
                dst = bank(2 + n % 2)
                for k in range(KE):
                    t = put("pe", lambda e, m=m, half=half, k=k, dst=dst: e.matmul(
                        dst, wqkv[:, k, m * P:(m + 1) * P], xT2[:, k, half * CH:(half + 1) * CH],
                        start=(k == 0), stop=(k == KE - 1)), pe_qkv, opt(t_xT, t_wb, free[n % 2]))
                to = (q2 if m < KE else k2)[:, m % KE, half * CH:(half + 1) * CH]
                sc = QSCALE if m < KE else 1.0
                free[n % 2] = put("dve", lambda e, m=m, dst=dst, to=to, sc=sc: e.tensor_scalar(
                    to, dst, bqkv[:, m:m + 1], sc, ALU.add, ALU.mult), dve_qkv, [t])
                n += 1
            if m < KE:
                for j in range(P // HD):
                    t_qm = put("dve", lambda e, m=m, j=j: e.tensor_scalar_mul(
                        qm[:, m * (P // HD) + j], q2[:, m], hmask[:, j:j + 1]), dve_qkv, [free[0], free[1]])
        for i in range(TT):
            dst = bank(2 + n % 2)[:, 0:EMB]
            for k in range(KE):
                t = put("pe", lambda e, i=i, k=k, dst=dst: e.matmul(
                    dst, xT2[:, k, i * P:(i + 1) * P], wqkv[:, k, 2 * EMB:3 * EMB],
                    start=(k == 0), stop=(k == KE - 1)), pe_qkv, opt(t_xT, t_wb, free[n % 2]))
            free[n % 2] = put("dve", lambda e, i=i, dst=dst: e.tensor_copy(
                vals2[:, i].rearrange("p (h w) -> p h w", w=VW)[:, :, 0:HD],
                dst.rearrange("p (h w) -> p h w", w=HD)), dve_qkv, [t, t_vones])
            n += 1
        qkv_done = [free[0], free[1], t_qm, t_vones]

        pe_s2, dve_s2, act_s2, pe_t2, act_t2, dve_t2, pe_v2 = (counter(n) for n in (
            "pe_s2", "dve_s2", "act_s2", "pe_t2", "act_t2", "dve_t2", "pe_v2"))
        s_read = [None, None]
        t_read = [None, None]
        w_read = [None, None]
        wT_read = [None, None]
        soft = {}

        def softmax2(u):
            b, hg, qt = u // 8, (u // 2) % 4, u % 2
            i = u % 2
            at = b * SEQ + qt * (SEQ - WIN)
            tok = b * SEQ + qt * P
            dst = bank(2 * i, 2).rearrange("p (h w) -> p h w", h=GH)[:, :, 0:WIN]
            for j in range(GH):
                h = hg * GH + j
                t = put("pe", lambda e, j=j, h=h: e.matmul(
                    dst[:, j], qm[:, h, tok:tok + P], k2[:, h // (P // HD), at:at + WIN], start=True, stop=True),
                    pe_s2, opt(s_read[i]) + qkv_done)
            s_read[i] = t = put("dve", lambda e: e.tensor_tensor(
                biased[i], dst, wmask[:, qt:qt + 1].broadcast_to([P, GH, WIN]), ALU.add), dve_s2, opt(t, w_read[i]))
            t = put("dve", lambda e: e.tensor_reduce(nmax[i], biased[i], AX_X, ALU.max, negate=True), dve_s2, [t])
            for j in range(GH):
                t2 = put("act", lambda e, j=j: e.activation(wt2[i][:, j], biased[i][:, j], ACT.Exp,
                                                            bias=nmax[i][:, j:j + 1]), act_s2, opt(t, w_read[i]))
            soft[u] = t2

        def weigh2(u):
            b, hg, qt = u // 8, (u // 2) % 4, u % 2
            i = u % 2
            full, edge = ((0, P), (P, 0)) if qt == 0 else ((HALF, P), (0, P - HALF))
            ft, et = 2 * b + qt, 2 * b + 1 - qt
            lo = edge[1]
            for j in range(GH):
                put("pe", lambda e, j=j: e.matmul(bank(4)[:, j * P:(j + 1) * P], wt2[i][:, j, full[0]:full[0] + P],
                                                  identf, start=True, stop=True), pe_t2, opt(soft[u], t_read[0]))
            t_a = (pe_t2, pe_t2.value)
            for j in range(GH):
                t = put("pe", lambda e, j=j: e.matmul(bank(5)[lo:lo + HALF, j * P:(j + 1) * P],
                                                      wt2[i][:, j, edge[0]:edge[0] + HALF],
                                                      identf, start=True, stop=True), pe_t2, opt(t_read[1]))
            w_read[i] = t
            t_read[0] = ta = put("act", lambda e: e.activation(wTa[i], bank(4), ACT.Copy), act_t2,
                                 opt(t_a, wT_read[i]))
            t_read[1] = tb = put("dve", lambda e: e.tensor_copy(wTb[i][lo:lo + HALF], bank(5)[lo:lo + HALF]),
                                 dve_t2, opt(t, wT_read[i]))
            o = bank(O_BANK)
            for j in range(GH):
                h = hg * GH + j
                put("pe", lambda e, j=j, h=h: e.matmul(
                    o[32 * j:32 * j + VW, qt * P:(qt + 1) * P], vals2[:, ft, h * VW:(h + 1) * VW],
                    wTa[i][:, j * P:(j + 1) * P], start=True, stop=False), pe_v2, opt(ta, o_read[0]) + qkv_done)
            for j in range(GH):
                h = hg * GH + j
                t = put("pe", lambda e, j=j, h=h: e.matmul(
                    o[32 * j:32 * j + VW, qt * P:(qt + 1) * P], vals2[lo:lo + HALF, et, h * VW:(h + 1) * VW],
                    wTb[i][lo:lo + HALF, j * P:(j + 1) * P], start=False, stop=True,
                    tile_position=(lo, 32 * j)), pe_v2, [tb])
            wT_read[i] = t
            if qt == 1:
                end_copy(t)
                end_norm(hg, bv2)
                if hg == NG - 1:
                    out_project(b, 0, wo2)
                    out_project(b, 1, wo2)

        UNITS = BATCH * NG * 2
        for u in range(UNITS + 1):
            if u < UNITS:
                softmax2(u)
            if u:
                weigh2(u - 1)

        fresh = phase_end()
        top[0] = kept
        xn3 = carve((TT, EMB))
        xT3 = carve((KE, TOK))
        wr = carve((KE, BANKS))
        br = carve((BANKS,))
        b2 = carve((EMB,))
        bank_no = carve((BANKS,))
        tile_size = carve((TT,))
        tile_no = carve((SLOT_TILES,))
        before = carve((P,))
        ones = carve((P,))
        logit = carve((TT, BANKS))
        lmax = carve((TT,))
        prob = carve((TT, BANKS))
        psumr = carve((TT,))
        prec = carve((TT,))
        top8 = carve((TT, 8))
        idx8 = carve((TT, 8), U32)
        idxf = carve((TT, 2))
        hot = [carve((TT, BANKS)) for _ in range(2)]
        padded = carve((2 * TT, BANKS))
        both = padded[:, TT:]
        gate = carve((TT, BANKS))
        gtmp = carve((TT, BANKS))
        gT = carve((TOK,))
        cmp = carve((BANKS, TT))
        tiles = carve((BANKS,))
        ends = [carve((BANKS,)) for _ in range(2)]
        start = carve((BANKS,))
        slot_of = carve((TT, BANKS))
        slotf = carve((2, TT))
        slot = carve((2, TT), U32)
        past = carve((SLOT_TILES, BANKS))
        ownerf = carve((SLOT_TILES,))
        owner = carve((SLOT_TILES,), I32)
        RING = 5
        w1s = [carve((KE, HID)) for _ in range(RING)]
        w2s = [carve((HC, EMB)) for _ in range(RING)]
        b1s = [carve((HC,)) for _ in range(RING)]
        xin = [carve((EMB,)) for _ in range(RING)]
        xTt = [carve((KE, P)) for _ in range(2)]
        hid = [carve((HC, P)) for _ in range(2)]
        yout = [carve((EMB,)) for _ in range(3)]
        picked = [carve((EMB,)) for _ in range(4)]

        ld_c = counter("ld_c")
        for dst, src in ((wr, "Wr"), (br, "br"), (b2[0:BANKS], "b2"), (bank_no, "bank_no"),
                         (tile_size, "tile_size"), (tile_no, "tile_no"), (before, "before"), (ones, "ones")):
            t_wc = dma("sp", dst, a[src], ld_c, fresh)
        layernorm_T(xT3, xn3, fresh, (0, 1))
        t_xT = (act_lnT, act_lnT.value)
        pe_r, dve_r, act_r = counter("pe_r"), counter("dve_r"), counter("act_r")

        def over_tiles(v):
            return v.rearrange("p (o e) -> p o e", o=1).broadcast_to([P, TT, BANKS])

        def over_banks(v):
            return v.rearrange("p (t o) -> p t o", o=1).broadcast_to([P, TT, BANKS])

        for i in range(TT):
            for k in range(KE):
                t = put("pe", lambda e, i=i, k=k: e.matmul(bank(2)[:, i * BANKS:(i + 1) * BANKS],
                                                           xT3[:, k, i * P:(i + 1) * P], wr[:, k],
                                                           start=(k == 0), stop=(k == KE - 1)), pe_r, [t_xT, t_wc])
        lgp = bank(2)[:, 0:TT * BANKS].rearrange("p (t e) -> p t e", t=TT)
        t = put("dve", lambda e: e.tensor_tensor(logit, lgp, over_tiles(br), ALU.add), dve_r, [t])
        t = put("dve", lambda e: e.reduce_max(lmax, logit, AX_X), dve_r, [t])
        t = put("dve", lambda e: e.tensor_tensor(logit, logit, over_banks(lmax), ALU.subtract), dve_r, [t])
        t = put("act", lambda e: e.activation(prob, logit, ACT.Exp), act_r, [t])
        t = put("dve", lambda e: e.reduce_sum(psumr, prob, AX_X), dve_r, [t])
        t = put("dve", lambda e: e.reciprocal(prec, psumr), dve_r, [t])
        t = put("dve", lambda e: e.tensor_tensor(prob, prob, over_banks(prec), ALU.mult), dve_r, [t])
        t_top = [put("dve", lambda e, i=i: e.max(top8[:, i], prob[:, i]), dve_r, [t]) for i in range(TT)]
        for i in range(TT):
            t = put("dve", lambda e, i=i: e.max_index(idx8[:, i], top8[:, i], prob[:, i]), dve_r, [t_top[i]])
        t = put("dve", lambda e: e.tensor_copy(idxf, idx8[:, :, 0:2]), dve_r, [t])
        for c in range(2):
            t_hot = put("dve", lambda e, c=c: e.tensor_tensor(hot[c], over_tiles(bank_no), over_banks(idxf[:, :, c]),
                                                              ALU.is_equal), dve_r, [t, t_wc])
        t_pad = put("dve", lambda e: e.memset(padded[:, 0:TT], 0.0), dve_r, fresh)
        t_both = put("dve", lambda e: e.tensor_tensor(both, hot[0], hot[1], ALU.add), dve_r, [t_hot])

        flat = padded.rearrange("p t e -> p (t e)")
        wide = TT * BANKS
        rank = bank(3)[:, 0:TT * BANKS]
        put("pe", lambda e: e.matmul(rank, before, flat[:, wide:], start=True, stop=False), pe_r,
            [t_pad, t_both, t_wc])
        for d in range(1, TT):
            t_rank = put("pe", lambda e, d=d: e.matmul(rank, ones, flat[:, wide - d * BANKS:2 * wide - d * BANKS],
                                                       start=False, stop=(d == TT - 1)), pe_r)
        counts = bank(4)[:, 0:BANKS]
        for i in range(TT):
            t = put("pe", lambda e, i=i: e.matmul(counts, ones, both[:, i], start=(i == 0), stop=(i == TT - 1)), pe_r)
        t = put("dve", lambda e: e.tensor_tensor(
            cmp, counts.rearrange("p (e o) -> p e o", o=1).broadcast_to([P, BANKS, TT]),
            tile_size.rearrange("p (o t) -> p o t", o=1).broadcast_to([P, BANKS, TT]), ALU.is_gt), dve_r, [t])
        t = put("dve", lambda e: e.reduce_sum(tiles, cmp, AX_X), dve_r, [t])
        src = tiles
        for n, d in enumerate((1, 2, 4, 8)):
            dst = ends[n % 2]
            put("dve", lambda e, src=src, dst=dst, d=d: e.tensor_copy(dst[:, 0:d], src[:, 0:d]), dve_r, [t])
            t = put("dve", lambda e, src=src, dst=dst, d=d: e.tensor_tensor(
                dst[:, d:], src[:, d:], src[:, 0:BANKS - d], ALU.add), dve_r, [t])
            t = (dve_r, dve_r.value)
            src = dst
        t_ends, last_tile = t, src
        t = put("dve", lambda e: e.tensor_tensor(start, last_tile, tiles, ALU.subtract), dve_r, [t])
        t = put("dve", lambda e: e.tensor_scalar_mul(start, start, float(P)), dve_r, [t])
        t = put("dve", lambda e: e.tensor_tensor(slot_of, rank.rearrange("p (t e) -> p t e", t=TT),
                                                 over_tiles(start), ALU.add), dve_r, [t, t_rank])
        for c in range(2):
            t = put("dve", lambda e, c=c: e.tensor_tensor(gtmp, slot_of, hot[c], ALU.mult), dve_r, [t])
            t = put("dve", lambda e, c=c: e.reduce_sum(slotf[:, c], gtmp, AX_X), dve_r, [t])
        t_slot = put("dve", lambda e: e.tensor_copy(slot, slotf), dve_r, [t])
        t = put("dve", lambda e: e.tensor_tensor(
            past[0:1], last_tile[0:1].rearrange("p (o e) -> p o e", o=1).broadcast_to([1, SLOT_TILES, BANKS]),
            tile_no[0:1].rearrange("p (j o) -> p j o", o=1).broadcast_to([1, SLOT_TILES, BANKS]), ALU.is_le),
            dve_r, [t_ends])
        t = put("dve", lambda e: e.reduce_sum(ownerf[0:1], past[0:1], AX_X), dve_r, [t])
        t_owner = put("dve", lambda e: e.tensor_scalar_min(owner[0:1], ownerf[0:1], float(BANKS - 1)), dve_r, [t])
        t = put("dve", lambda e: e.tensor_tensor(gate, hot[0], over_banks(top8[:, :, 0]), ALU.mult), dve_r)
        t = put("dve", lambda e: e.tensor_tensor(gtmp, hot[1], over_banks(top8[:, :, 1]), ALU.mult), dve_r, [t])
        t_gate = put("dve", lambda e: e.tensor_tensor(gate, gate, gtmp, ALU.add), dve_r, [t])

        st_slot = counter("st_slot")
        for c in range(2):
            for i in range(TT):
                t_rows = put("pool", lambda e, c=c, i=i: e.indirect_dma_start(
                    scratch["slots_x"], bass.IndirectOffsetOnAxis(ap=slot[:, c, i:i + 1], axis=0), xn3[:, i], None),
                    st_slot, [t_slot, t_blank], 16)

        ld_w12 = [counter(f"ld_w12{i}") for i in range(RING)]
        ld_x = [counter(f"ld_x{i}") for i in range(RING)]
        pe_x, act_x, pe_h, act_h, dve_h, pe_y, dve_y = (counter(n) for n in (
            "pe_x", "act_x", "pe_h", "act_h", "dve_h", "pe_y", "dve_y"))
        st_y = [counter(f"st_y{i}") for i in range(3)]
        w_in, x_in, xT_in, h_in, y_out = {}, {}, {}, {}, {}
        turned, up_pe, down_pe = {}, {}, {}

        def load_tile(j):
            i = j % RING

            def weights(e):
                owns = e.value_load(owner[0:1, j:j + 1], min_val=0, max_val=BANKS - 1)
                e.dma_start(w1s[i], a["W1"][bass.ds(owns, 1)].rearrange("o p k n -> p (o k) n")).then_inc(
                    ld_w12[i].sem, 16)
                e.dma_start(w2s[i], a["W2"][bass.ds(owns, 1)].rearrange("o p k n -> p (o k) n")).then_inc(
                    ld_w12[i].sem, 16)
                return e.dma_start(b1s[i], a["b1"][bass.ds(owns, 1)].rearrange("o p k -> p (o k)"))

            ld_w12[i].value += 32
            w_in[j] = put("sp", weights, ld_w12[i], opt(t_owner, down_pe.get(j - RING)), 16)

        def load_rows(j):
            x_in[j] = dma("act", xin[j % RING], scratch["slots_x"][j * P:(j + 1) * P], ld_x[j % RING],
                          opt(t_rows, turned.get(j - RING)))

        def turn(j):
            dst = bank(6 + j % 2)[:, 0:KE * P]
            for k in range(KE):
                t = put("pe", lambda e, k=k: e.matmul(dst[:, k * P:(k + 1) * P], xin[j % RING][:, k * P:(k + 1) * P],
                                                      identf, start=True, stop=True), pe_x,
                        opt(x_in[j], xT_in.get(j - 2)))
            turned[j] = t
            xT_in[j] = put("dve", lambda e: e.tensor_copy(xTt[j % 2].rearrange("p k t -> p (k t)"), dst), act_x,
                           opt(t, up_pe.get(j - 2)))

        def up(j):
            for hb in range(2):
                dst = bank(2 * (j % 2) + hb)
                for q in range(HC // 2):
                    hc = hb * (HC // 2) + q
                    for k in range(KE):
                        t = put("pe", lambda e, k=k, q=q, hc=hc, dst=dst: e.matmul(
                            dst[:, q * P:(q + 1) * P], w1s[j % RING][:, k, hc * P:(hc + 1) * P], xTt[j % 2][:, k],
                            start=(k == 0), stop=(k == KE - 1)), pe_h,
                            opt(w_in[j], xT_in[j], *h_in.get(j - 2, ())))
                ws = opt(t, down_pe.get(j - 2))
                for q in range(HC // 2):
                    hc = hb * (HC // 2) + q
                    src = dst[:, q * P:(q + 1) * P]
                    if hb:
                        t_d = put("dve", lambda e, hc=hc, src=src: e.tensor_scalar(
                            hid[j % 2][:, hc], src, b1s[j % RING][:, hc:hc + 1], 0.0, ALU.add, ALU.max), dve_h, ws)
                    else:
                        t_a = put("act", lambda e, hc=hc, src=src: e.activation(
                            hid[j % 2][:, hc], src, ACT.Relu, bias=b1s[j % RING][:, hc:hc + 1]), act_h, ws)
            up_pe[j] = t
            h_in[j] = (t_a, t_d)

        def down(j):
            dst = bank(4 + j % 2)[:, 0:EMB]
            for hc in range(HC):
                t = put("pe", lambda e, hc=hc: e.matmul(dst, hid[j % 2][:, hc], w2s[j % RING][:, hc],
                                                        start=(hc == 0), stop=(hc == HC - 1)), pe_y,
                        opt(*h_in[j], y_out.get(j - 2)))
            down_pe[j] = t
            i = j % 3
            y_out[j] = put("dve", lambda e: e.tensor_copy(yout[i], dst), dve_y,
                           opt(t, (st_y[i], st_y[i].value)))
            dma("act", scratch["slots_y"][j * P:(j + 1) * P], yout[i], st_y[i], [y_out[j]])

        for j in range(RING):
            load_tile(j)
        for j in range(3):
            load_rows(j)
        for s in range(SLOT_TILES + 2):
            if s < SLOT_TILES:
                turn(s)
                if s + 3 < SLOT_TILES:
                    load_rows(s + 3)
            if 1 <= s < SLOT_TILES + 1:
                up(s - 1)
            if s >= 2:
                down(s - 2)
                if s - 2 + RING < SLOT_TILES:
                    load_tile(s - 2 + RING)

        for i in range(TT):
            t = put("pe", lambda e, i=i: e.matmul(bank(i // 4)[0:BANKS, (i % 4) * P:(i % 4 + 1) * P], gate[:, i],
                                                  identf, start=True, stop=True), pe_r,
                    [t_gate, (act_h, act_h.value), (dve_h, dve_h.value)])
        t_gT = put("dve", lambda e: e.tensor_copy(gT[0:BANKS], bank(0, 2)[0:BANKS]), dve_r, [t])
        pe_o, dve_o, st_o = counter("pe_o"), counter("dve_o"), counter("st_o")
        ld_y = [counter(f"ld_y{i}") for i in range(4)]
        written = [(c, c.value) for c in st_y]
        used = [None] * 4
        b_read = [None, None]
        n = 0
        for i in range(TT):
            got = []
            for c in range(2):
                r = n % 4
                n += 1
                got.append((r, put("pool", lambda e, c=c, i=i, r=r: e.indirect_dma_start(
                    picked[r], None, scratch["slots_y"], bass.IndirectOffsetOnAxis(ap=slot[:, c, i:i + 1], axis=0)),
                    ld_y[r], opt(t_slot, used[r], *written), 16)))
            dst = bank(2 + i % 2)[:, 0:EMB]
            t = put("pe", lambda e, i=i, dst=dst: e.matmul(dst, gT[0:BANKS, i * P:(i + 1) * P], b2[0:BANKS],
                                                           start=True, stop=True), pe_o, opt(t_gT, b_read[i % 2]))
            b_read[i % 2] = t = put("dve", lambda e, i=i, dst=dst: e.tensor_tensor(x[:, i], dst, x[:, i], ALU.add),
                                    dve_o, [t])
            for c in range(2):
                r, t_y = got[c]
                used[r] = t = put("dve", lambda e, i=i, c=c, r=r: e.scalar_tensor_tensor(
                    x[:, i], picked[r], top8[:, i, c:c + 1], x[:, i], ALU.mult, ALU.add), dve_o, [t, t_y])
            dma("sp", out[:, i], x[:, i], st_o, [t])
        put("sp", None, None, [(st_o, st_o.value)])

        block = ctx.enter_context(nc.Block())

        def play(name, e):
            for waits, make, sem, by in queue[name]:
                for s, v in waits:
                    e.wait_ge(s, v)
                if make is not None:
                    i = make(e)
                    if sem is not None:
                        i.then_inc(sem, by)

        @block.tensor
        def _(e):
            play("pe", e)

        @block.scalar
        def _(e):
            play("act", e)

        @block.vector
        def _(e):
            play("dve", e)

        @block.gpsimd
        def _(e):
            play("pool", e)

        @block.sync
        def _(e):
            play("sp", e)


def layouts(i):
    f = np.float32

    def rows(w, k, p=P):
        return np.ascontiguousarray(w.reshape(k, p, -1).transpose(1, 0, 2))

    def by_head(w):
        w = w.reshape(NG, GH, HD, -1)
        o = np.zeros((NG, GH, 32, w.shape[-1]), f)
        o[:, :, :HD] = w
        return np.ascontiguousarray(o.reshape(NG, P, -1).transpose(1, 0, 2))

    def spread(v):
        return np.ascontiguousarray(np.broadcast_to(v, (P,) + v.shape))

    q = np.arange(P)[:, None, None]
    j = np.arange(WIN)[None, None, :]
    t = np.arange(2)[None, :, None]
    dist = np.abs(P * t + q - ((SEQ - WIN) * t + j))
    p = np.arange(P)
    bqkv = i["L0_attn_b_qkv"]
    return {
        "x": rows(i["x"].reshape(TOK, EMB), TT),
        "ctxT": np.ascontiguousarray(i["ctx_768"].reshape(BATCH, KV, 2, KC).transpose(0, 3, 2, 1)),
        "wqT": rows(i["L0_xattn_wq"].T, KE),
        "wkT": rows(i["L0_xattn_wk"].T, 2, KC),
        "wvT": rows(i["L0_xattn_wv"].T, 2, KC),
        "woT": by_head(i["L0_xattn_wo"].T),
        "bq": np.ascontiguousarray(i["L0_xattn_bq"].reshape(KE, P).T),
        "bk": np.ascontiguousarray(i["L0_xattn_bk"].reshape(KE, P).T),
        "bv": by_head(i["L0_xattn_bv"])[:, :, 0].copy(),
        "bo": spread(i["L0_xattn_bo"]),
        "w_qkv": rows(i["L0_attn_w_qkv"], KE),
        "w_out": by_head(i["L0_attn_w_out"]),
        "b_qk": np.ascontiguousarray(bqkv[:2 * EMB].reshape(2 * KE, P).T),
        "b_v": by_head(bqkv[2 * EMB:])[:, :, 0].copy(),
        "b_out": spread(i["L0_attn_b_out"]),
        "Wr": rows(i["L0_ffn_Wr"], KE),
        "br": spread(i["L0_ffn_br"]),
        "W1": np.ascontiguousarray(i["L0_ffn_W1"].reshape(BANKS, KE, P, HID).transpose(0, 2, 1, 3)),
        "b1": np.ascontiguousarray(i["L0_ffn_b1"].reshape(BANKS, HC, P).transpose(0, 2, 1)),
        "W2": np.ascontiguousarray(i["L0_ffn_W2"].reshape(BANKS, HC, P, EMB).transpose(0, 2, 1, 3)),
        "b2": i["L0_ffn_b2"],
        "identf": np.eye(P, dtype=f),
        "lsel": (p[:, None] == (p[None, :] // 32) * 32 + HD).astype(f),
        "wmask": np.where(dist <= HALF, f(0), f(-3e38)).astype(f),
        "hmask": (p[:, None] // HD == np.arange(P // HD)[None, :]).astype(f),
        "bank_no": spread(np.arange(BANKS, dtype=f)),
        "tile_size": spread(P * np.arange(TT, dtype=f)),
        "tile_no": spread(np.arange(SLOT_TILES, dtype=f)),
        "before": (p[:, None] < p[None, :]).astype(f),
        "ones": np.ones((P, P), f),
    }


def kernel(**inputs):
    import concourse.bacc as bacc
    from concourse.bass_utils import run_bass_kernel_spmd

    nc = bacc.Bacc("TRN2", target_bir_lowering=False, num_devices=1)
    arrays, aps = {}, {}
    for name, v in layouts({k: np.asarray(v) for k, v in inputs.items()}).items():
        arrays[f"in_{name}"] = v
        aps[name] = nc.dram_tensor(f"in_{name}", v.shape, mybir.dt.from_np(v.dtype), kind="ExternalInput").ap()
    out = nc.dram_tensor("out", (P, TT, EMB), F32, kind="ExternalOutput").ap()
    scratch = {"qparts": nc.dram_tensor("qparts", (3, EMB, TOK), BF16, kind="Internal").ap()}
    for name in ("slots_x", "slots_y"):
        scratch[name] = nc.dram_tensor(name, (SLOT_TILES * P, EMB), F32, kind="Internal").ap()
    build(nc, aps, out, scratch)
    r = run_bass_kernel_spmd(nc, [arrays], core_ids=[0])
    return np.ascontiguousarray(r.results[0]["out"].transpose(1, 0, 2)).reshape(BATCH, SEQ, EMB)
```

```python
from contextlib import ExitStack

import numpy as np

import concourse.bass as bass
from concourse import mybir

F32 = mybir.dt.float32
BF16 = mybir.dt.bfloat16
U32 = mybir.dt.uint32
I32 = mybir.dt.int32
ACT = mybir.ActivationFunctionType
ALU = mybir.AluOpType
AX_X = mybir.AxisListType.X

P = 128
WORDS = 53000
BATCH, SEQ, EMB = 4, 256, 256
KV, CTX = 4096, 192
HEADS, HD = 16, 16
TOK = BATCH * SEQ
TT = TOK // P
KE = EMB // P
KC = CTX // 2
GH = 4
GROUPS = BATCH * HEADS // GH
NG = HEADS // GH
KT = KV // P
CH = 512
NCH = KV // CH
VW = HD + 1
SLOTS = 6
K_PART = (0, 0, 0, 1, 1, 2)
Q_PART = (0, 1, 2, 0, 1, 0)
STK = SLOTS * HD
ROWS = STK + 3
QSCALE = 1.0 / HD ** 0.5
EPS = 1e-5
ROOT_BITS = float(0x5F3759DF)
NW = 3
HALF = 32
WIN = P + HALF
BANKS, HID, NSEL = 16, 1024, 2
HC = HID // P
SLOT_TILES = NSEL * TOK // P + BANKS - 1


class Counter:

    def __init__(self, sem):
        self.sem, self.value = sem, 0


def build(nc, a, out, scratch):
    ctx = ExitStack()
    with ctx:
        def counter(name):
            return Counter(ctx.enter_context(nc.semaphore(name)))

        queue = {n: [] for n in ("pe", "act", "dve", "pool", "sp")}
        waited = {n: {} for n in queue}
        every = []

        def put(engine, make, sem, after=(), by=1):
            waits = []
            for c, v in after:
                if waited[engine].get(c, 0) < v:
                    waited[engine][c] = v
                    waits.append((c.sem, v))
            if sem is not None:
                sem.value += by
                if sem not in every:
                    every.append(sem)
            queue[engine].append((waits, make, sem.sem if sem else None, by))
            return (sem, sem.value) if sem else None

        def dma(engine, dst, src, sem, after=()):
            return put(engine, lambda e, d=dst, s=src: e.dma_start(d, s), sem, after, 16)

        def phase_end():
            return [(c, c.value) for c in every]

        arena = ctx.enter_context(nc.sbuf_tensor("arena", [P, WORDS], F32))
        top = [0]

        def carve(shape, dt=F32):
            n = int(np.prod(shape)) * (2 if dt == BF16 else 4)
            n = (n + 3) // 4
            v = arena[:, top[0]:top[0] + n]
            top[0] += n
            assert top[0] <= WORDS, top[0]
            if dt != F32:
                v = v.bitcast(dt)
            if len(shape) == 2:
                v = v.rearrange("p (a b) -> p a b", a=shape[0])
            elif len(shape) == 3:
                v = v.rearrange("p (a b c) -> p a b c", a=shape[0], b=shape[1])
            return v

        psum = ctx.enter_context(nc.psum_tensor("psum", [P, 8 * 512], F32))

        S_BANKS = (0, 2)
        M_BANKS = (4, 5)
        X_BANK, O_BANK = 6, 7

        def bank(i, n=1):
            return psum[:, i * 512:(i + n) * 512]

        x = carve((TT, EMB))
        identf = carve((P,))
        identb = carve((P,), BF16)
        lsel = carve((P,))
        stats = carve((TT, 6))
        mv = carve((TT, 2))
        rstd = carve((TT,))
        rtmp = carve((2, TT))
        o_raw = carve((SEQ,))
        o_norm = carve((NG, SEQ))
        kept = top[0]

        ld_const = counter("ld_const")
        dve_ln = counter("dve_ln")
        pe_lnT = counter("pe_lnT")
        act_lnT = counter("act_lnT")

        dma("sp", x, a["x"], ld_const)
        t_const = dma("sp", identf, a["identf"], ld_const)
        t_identb = put("dve", lambda e: e.tensor_copy(identb, identf), dve_ln, [t_const])

        def layernorm(xn, after, tiles=range(TT)):
            sl = slice(tiles[0], tiles[-1] + 1)
            var, sq, r = rtmp[:, 0, sl], rtmp[:, 1, sl], rstd[:, sl]
            done = {}

            def statistics():
                for i in tiles:
                    t = put("dve", lambda e, i=i: e.bn_stats(stats[:, i, :], x[:, i, :]), dve_ln, after)
                for i in tiles:
                    t2 = put("dve", lambda e, i=i: e.bn_aggr(mv[:, i, :], stats[:, i, :]), dve_ln, [t])
                done[0] = put("dve", lambda e: e.tensor_scalar_add(var, mv[:, sl, 1], EPS), dve_ln, [t2])

            def root():
                t = put("dve", lambda e: e.tensor_scalar(r.bitcast(I32), var.bitcast(I32), -0.5, ROOT_BITS,
                                                         ALU.mult, ALU.add), dve_ln, [done[0]])
                for _ in range(3):
                    t = put("dve", lambda e: e.tensor_tensor(sq, r, r, ALU.mult), dve_ln, [t])
                    t = put("dve", lambda e: e.tensor_tensor(sq, sq, var, ALU.mult), dve_ln, [t])
                    t = put("dve", lambda e: e.tensor_scalar(sq, sq, -0.5, 1.5, ALU.mult, ALU.add), dve_ln, [t])
                    t = put("dve", lambda e: e.tensor_tensor(r, r, sq, ALU.mult), dve_ln, [t])
                done[1] = t

            def apply():
                return [put("dve", lambda e, i=i: e.tensor_scalar(
                    xn[:, i, :], x[:, i, :], mv[:, i, 0:1], rstd[:, i:i + 1], ALU.subtract, ALU.mult), dve_ln,
                    [done[1], *after]) for i in tiles]

            return [statistics, root, apply]

        def all_of(steps):
            for step in steps:
                last = step()
            return last

        def turn_rows(xT, xn, norm, banks):
            n = 0
            evac = [None] * 2
            for k in range(KE):
                for half in range(TT // 4):
                    dst = bank(banks[n % 2])
                    for j in range(4):
                        i = 4 * half + j
                        w = [norm[i], t_const] + ([evac[n % 2]] if evac[n % 2] else [])
                        t = put("pe", lambda e, i=i, j=j, k=k, dst=dst: e.transpose(
                            dst[:, j * P:(j + 1) * P], xn[:, i, k * P:(k + 1) * P], identf), pe_lnT, w)
                    evac[n % 2] = put("act", lambda e, k=k, half=half, dst=dst: e.activation(
                        xT[:, k, half * CH:(half + 1) * CH], dst, ACT.Copy), act_lnT, [t])
                    n += 1
            return evac[1]

        kstack = [carve((GH, KV), BF16) for _ in range(3)]
        early_at = top[0] - 2 * GH * KV // 2
        setup_at = top[0] - 2 * GH * KV // 2
        pieces = carve((3, KV), BF16)
        vals = carve((KT, HEADS * VW))
        ctx_in = [carve((2, CH)) for _ in range(2)]
        ctx_first = vals.rearrange("p t v -> p (t v)")[0:KC, 0:2 * KV].rearrange("p (c k n) -> p c k n", c=NCH, k=2)
        wts = [carve((GH * SEQ,)) for _ in range(NW)]
        qstack = [carve((GH, SEQ), BF16) for _ in range(3)]
        rest = [carve((CH,)) for _ in range(2)]
        wk = carve((2, EMB))
        wv = carve((2, EMB))
        wo = carve((NG, EMB))
        bk = carve((KE,))
        bv = carve((NG,))
        bq = carve((KE,))
        part_max = carve((GH * 2, NCH))
        neg_max = carve((GH * 2,))
        neg_rest = carve((GH * 2,))
        neg_parts = carve((3, GH * 2), BF16)
        keep_top, top[0] = top[0], setup_at
        xn1 = carve((TT, EMB))
        xT1 = carve((KE, TOK))
        wq = carve((KE, EMB))
        qf = carve((KE, TOK))
        bo_bc = carve((EMB,))
        qparts = carve((3, KE, TOK), BF16)
        qrest = carve((CH,))
        assert top[0] <= setup_at + 2 * GH * KV // 2
        top[0] = keep_top

        ld_wk, ld_w = counter("ld_wk"), counter("ld_w")
        dma("sp", wk[0:KC], a["wkT"], ld_wk)
        t_wk = dma("sp", bk, a["bk"], ld_wk)
        ld_first = [counter(f"ld_first{c}") for c in range(NCH)]
        first_in = [dma("sp", ctx_first[:, c], a["ctxT"][0, :, :, c * CH:(c + 1) * CH], ld_first[c])
                    for c in range(NCH)]
        dma("sp", wq, a["wqT"], ld_w)
        dma("sp", wv[0:KC], a["wvT"], ld_w)
        for dst, src in ((lsel, "lsel"), (wo, "woT"), (bv, "bv"), (bq, "bq"), (bo_bc, "bo")):
            t_w = dma("sp", dst, a[src], ld_w)

        pool_set = counter("pool_set")
        t_vones = []
        t_ones = [put("pool", lambda e: e.memset(kstack[0][STK:ROWS], 1.0), pool_set)]
        dve_set = counter("dve_set")
        t_zero = put("dve", lambda e: e.memset(bank(O_BANK), 0.0), dve_set)
        pe_q, dve_q, pool_bias = counter("pe_q"), counter("dve_q"), counter("pool_bias")
        st_q = [counter("st_q0"), counter("st_q1")]
        q_read = {}
        setup = {}

        def normalise():
            setup["rows"] = all_of(layernorm(xn1, [t_const]))

        def project_q(half):
            if half == 0:
                setup["xT"] = turn_rows(xT1, xn1, setup["rows"], (0, 1))
            sl = slice(half * CH, (half + 1) * CH)
            for m in range(KE):
                dst = bank(2 + m)
                for k in range(KE):
                    t = put("pe", lambda e, m=m, k=k, dst=dst: e.matmul(
                        dst, wq[:, k, m * P:(m + 1) * P], xT1[:, k, sl], start=(k == 0), stop=(k == KE - 1)),
                        pe_q, opt(setup["xT"], t_w, q_read.get(m)))
                q_read[m] = t = put("dve", lambda e, m=m, dst=dst: e.tensor_scalar(
                    qf[:, m, sl], dst, bq[:, m:m + 1], QSCALE, ALU.add, ALU.mult), dve_q, [t])
                t = put("dve", lambda e, m=m: e.tensor_copy(qparts[:, 0, m, sl], qf[:, m, sl]), dve_q, [t])
                t = put("dve", lambda e, m=m: e.tensor_tensor(
                    qrest, qf[:, m, sl], qparts[:, 0, m, sl], ALU.subtract), dve_q, [t, (dve_q, dve_q.value)])
                t = put("dve", lambda e, m=m: e.tensor_copy(qparts[:, 1, m, sl], qrest), dve_q, [t])
                t = put("dve", lambda e, m=m: e.tensor_tensor(
                    qparts[:, 2, m, sl], qrest, qparts[:, 1, m, sl], ALU.subtract), dve_q, [t])
            qd = scratch["qparts"].rearrange("s (k p) t -> s p k t", p=P)
            for s in range(3):
                setup["q", half] = dma("sp", qd[s][:, :, sl], qparts[:, s, :, sl], st_q[half], [t])

        def end_setup():
            for i in range(TT):
                setup["bias"] = put("pool", lambda e, i=i: e.tensor_tensor(x[:, i, :], x[:, i, :], bo_bc, ALU.add),
                                    pool_bias, [t_w, (dve_ln, dve_ln.value), (pool_part, pool_part.value)])
            setup["done"] = [setup["q", 0], setup["q", 1], (dve_q, dve_q.value), (pe_q, pe_q.value), setup["bias"]]
            t_vones.append(put("pool", lambda e: e.memset(
                vals.rearrange("p t (h w) -> p t h w", w=VW)[:, :, :, HD], 1.0), pool_set,
                [(pe_proj, pe_proj.value), (pool_part, pool_part.value), t_ones[-1], setup["bias"]]))
            for s in (1, 2):
                t_ones.append(put("pool", lambda e, s=s: e.memset(kstack[s][STK:ROWS], 1.0), pool_set,
                                  setup["done"] + [t_vones[0], (pool_part, pool_part.value)]))

        pe_proj, pe_score, pe_max, pe_pv, pe_end = (counter(n) for n in ("pe_proj", "pe_score", "pe_max", "pe_pv", "pe_end"))
        act_hi, act_exp, act_val = counter("act_hi"), counter("act_exp"), counter("act_val")
        dve_rest, dve_max, dve_end, dve_neg = (counter(n) for n in ("dve_rest", "dve_max", "dve_end", "dve_neg"))
        act_neg, act_mid = counter("act_neg"), counter("act_mid")
        pool_part = counter("pool_part")
        ld_ctx = [counter(f"ld_ctx{i}") for i in range(len(ctx_in))]
        ld_k = [counter(f"ld_k{i}") for i in range(3)]
        ld_q = [counter(f"ld_q{i}") for i in range(3)]

        x_free = {}
        ctx_used = [None] * len(ctx_in)
        n_ctx = [0]
        ctx_now = [None]
        scores_done = {}
        exp_done = []
        pv_done = []
        max_used = [None, None]
        n_max = [0]
        pieces_read = [[]]
        pieces_ready = {}
        val_written = {}
        k_ready, q_ready, neg_ready = {}, {}, {}

        def opt(*t):
            return [v for v in t if v]

        chunks = []
        for s in range(-1, GROUPS):
            if s % 2 == 0 and s + 2 < GROUPS:
                chunks += [((s + 2) // NG, c) for c in range(NCH)]
            if s % NG == NG - 1 and (s + 1) // NG < BATCH:
                chunks += [((s + 1) // NG, c) for c in range(NCH)]
        loaded = []

        def load_ctx():
            n = len(loaded)
            if n < len(chunks):
                b, c = chunks[n]
                i = n % len(ctx_in)
                loaded.append(dma("act", ctx_in[i][0:KC], a["ctxT"][b, :, :, c * CH:(c + 1) * CH], ld_ctx[i],
                                  opt(ctx_used[i])))

        def next_ctx():
            n = n_ctx[0]
            n_ctx[0] += 1
            load_ctx()
            return n % len(ctx_in), loaded[n]

        load_ctx()

        def load_q(g):
            b, hg = divmod(g, NG)
            after = opt(scores_done.get(g - 3)) + [setup["q", b // 2]]
            for s in range(SLOTS):
                src = scratch["qparts"][Q_PART[s], hg * GH * HD:(hg + 1) * GH * HD, b * SEQ:(b + 1) * SEQ]
                t = dma("sp", qstack[g % 3][s * HD:(s + 1) * HD], src.rearrange("(h d) t -> d h t", d=HD),
                        ld_q[g % 3], after)
            q_ready[g] = t

        def scatter_k(g):
            after = opt(scores_done.get(g - 3), *pieces_ready[g // 2]) + (setup["done"] if g else [])
            row = (g % 2) * GH * HD
            for s in range(SLOTS):
                t = dma("sp", kstack[g % 3][s * HD:(s + 1) * HD], pieces[row:row + GH * HD, K_PART[s]],
                        ld_k[g % 3], after)
            k_ready[g] = t
            pieces_read[0] = opt(*pieces_read[0]) + [t]

        def project_k(mt, c, between=None):
            b, m = divmod(mt, 2)
            i, t_in = next_ctx() if mt else (None, first_in[c])
            src = ctx_in[i] if mt else ctx_first[:, c]
            xb = X_BANK if mt else (X_BANK, *M_BANKS)[c % 3]
            dst = bank(xb)
            for k in range(2):
                if k and between:
                    between()
                t = put("pe", lambda e, k=k: e.matmul(dst, wk[0:KC, k, m * P:(m + 1) * P], src[0:KC, k],
                                                      start=(k == 0), stop=(k == 1)),
                        pe_proj, opt(t_in, t_wk, x_free.get(xb)))
            if mt:
                ctx_used[i] = t
            sl = slice(c * CH, (c + 1) * CH)
            hi = pieces[:, 0, sl]
            t_hi = put("act", lambda e: e.activation(hi, dst, ACT.Identity, bias=bk[:, m:m + 1]), act_hi,
                       [t] + pieces_read[0])
            r = rest[c % 2]

            def split():
                t_r = put("dve", lambda e: e.scalar_tensor_tensor(r, dst, bk[:, m:m + 1], hi, ALU.add, ALU.subtract),
                          dve_rest, opt(t_hi, rest_used[c % 2]))
                x_free[xb] = t_r
                if mt:
                    t = put("pool", lambda e: e.tensor_copy(pieces[:, 1, sl], r), pool_part,
                            [t_r, (pool_set, pool_set.value)] + pieces_read[0])
                else:
                    max_used[0], max_used[1] = x_free.get(M_BANKS[0]), x_free.get(M_BANKS[1])
                    t = put("act", lambda e: e.activation(pieces[:, 1, sl], r, ACT.Copy), act_mid, [t_r])
                t = put("pool", lambda e: e.tensor_tensor(pieces[:, 2, sl], r, pieces[:, 1, sl], ALU.subtract),
                        pool_part, [t, (pool_set, pool_set.value)])
                rest_used[c % 2] = t
                pieces_ready[mt] = [t_hi, t]
                if c == NCH - 1:
                    scatter_k(2 * mt)

            later.append(split)

        rest_used = [None, None]
        later = []

        def project_v(b, t_):
            c, j = divmod(t_, CH // P)
            if j == 0:
                ctx_now[0] = next_ctx()
            i, t_in = ctx_now[0]
            xb = X_BANK if b or j % 2 else S_BANKS[0]
            dst = bank(xb)[:, 0:EMB]
            for k in range(2):
                t = put("pe", lambda e, k=k: e.matmul(dst, ctx_in[i][0:KC, k, j * P:(j + 1) * P], wv[0:KC, k],
                                                      start=(k == 0), stop=(k == 1)),
                        pe_proj, opt(t_in, t_w, x_free.get(xb)))
            if j == CH // P - 1:
                ctx_used[i] = t
            old = pv_done[(b * NG - 1) * KT + t_] if b else None
            x_free[xb] = val_written[b, t_] = put("act", lambda e: e.activation(
                vals[:, t_].rearrange("p (h w) -> p h w", w=VW)[:, :, 0:HD],
                dst.rearrange("p (h w) -> p h w", w=HD), ACT.Copy), act_val, opt(t, old, t_vones[0]))

        def max_task(g, n):
            hq, c = divmod(n, NCH)
            h, qt = divmod(hq, 2)
            i = n_max[0] % 2
            n_max[0] += 1
            dst = bank(M_BANKS[i])
            t = put("pe", lambda e: e.matmul(dst, qstack[g % 3][0:STK, h, qt * P:(qt + 1) * P],
                                             kstack[g % 3][0:STK, h, c * CH:(c + 1) * CH], start=True, stop=True),
                    pe_max, opt(k_ready[g], q_ready[g], max_used[i]))
            max_used[i] = put("dve", lambda e: e.reduce_max(part_max[:, hq, c:c + 1], dst, AX_X), dve_max,
                              opt(t, (dve_neg, dve_neg.value)))

        def max_end(g):
            t = put("dve", lambda e: e.tensor_reduce(neg_max, part_max, AX_X, ALU.max, negate=True), dve_neg,
                    [max_used[0], max_used[1]])
            t = put("dve", lambda e: e.tensor_copy(neg_parts[:, 0], neg_max), dve_neg, [t, (pe_end, pe_end.value)])
            t = put("dve", lambda e: e.tensor_tensor(neg_rest, neg_max, neg_parts[:, 0], ALU.subtract), dve_neg, [t])
            t = put("dve", lambda e: e.tensor_copy(neg_parts[:, 1], neg_rest), dve_neg, [t])
            t = put("dve", lambda e: e.tensor_tensor(neg_parts[:, 2], neg_rest, neg_parts[:, 1], ALU.subtract),
                    dve_neg, [t])
            neg_ready[g] = [t]

        def max_rows(g):
            both = bank(M_BANKS[0], 2)
            rows = qstack[g % 3][STK:ROWS].rearrange("p h t -> p (h t)")
            for i in range(2):
                for hq in range(GH * i, GH * i + GH):
                    t = put("pe", lambda e, hq=hq: e.matmul(both[STK:ROWS, hq * P:(hq + 1) * P], neg_parts[:, :, hq],
                                                            identb, start=True, stop=True),
                            pe_end, [neg_ready[g][0], max_used[0], max_used[1], t_identb])
                sl = slice(i * CH, (i + 1) * CH)
                if i:
                    t = put("act", lambda e, sl=sl: e.activation(rows[:, sl], both[STK:ROWS, sl], ACT.Copy),
                            act_neg, [t])
                else:
                    t = put("dve", lambda e, sl=sl: e.tensor_copy(rows[:, sl], both[STK:ROWS, sl]), dve_neg, [t])
                neg_ready[g].append(t)
            max_used[0], max_used[1] = neg_ready[g][1:]

        def scores(g, t_):
            n = g * KT + t_
            dst = bank(S_BANKS[n % 2], 2)
            w = opt(k_ready[g], *neg_ready[g], exp_done[n - 2] if n >= 2 else x_free.get(S_BANKS[0]),
                    t_ones[g % 3])
            for h in range(GH):
                t = put("pe", lambda e, h=h: e.matmul(dst[:, h * SEQ:(h + 1) * SEQ],
                                                      kstack[g % 3][0:ROWS, h, t_ * P:(t_ + 1) * P],
                                                      qstack[g % 3][0:ROWS, h], start=True, stop=True), pe_score, w)
            scores_done[g] = t
            exp_done.append(put("act", lambda e: e.activation(wts[n % NW], dst, ACT.Exp), act_exp,
                                opt(t, pv_done[n - NW] if n >= NW else None)))

        def weigh(g, t_):
            n = g * KT + t_
            b, hg = divmod(g, NG)
            w = opt(exp_done[n], val_written[b, t_], o_read[0], t_vones[0])
            for j in range(GH):
                h = hg * GH + j
                t = put("pe", lambda e, j=j, h=h: e.matmul(
                    bank(O_BANK)[32 * j:32 * j + VW, 0:SEQ], vals[:, t_, h * VW:(h + 1) * VW],
                    wts[n % NW][:, j * SEQ:(j + 1) * SEQ], start=(t_ == 0), stop=(t_ == KT - 1)), pe_pv, w)
            pv_done.append(t)

        o_read = [t_zero]
        norm_done = {}

        def end_copy(last):
            o_read[0] = put("act", lambda e: e.activation(o_raw, bank(O_BANK)[:, 0:SEQ], ACT.Copy), act_end,
                            opt(last, (pe_end, pe_end.value), (dve_end, dve_end.value)))

        def end_norm(hg, bias):
            xb = bank(X_BANK)[:, 0:SEQ]
            t = put("pe", lambda e: e.matmul(xb, lsel, o_raw, start=True, stop=True), pe_end,
                    opt(o_read[0], x_free[X_BANK]))
            x_free[X_BANK] = t = put("dve", lambda e: e.reciprocal(o_norm[:, hg], xb), dve_end,
                                [t, (pe_out, pe_out.value)])
            t = put("dve", lambda e: e.tensor_tensor(o_norm[:, hg], o_raw, o_norm[:, hg], ALU.mult), dve_end, [t])
            norm_done[hg] = put("dve", lambda e: e.tensor_scalar_add(o_norm[:, hg], o_norm[:, hg], bias[:, hg:hg + 1]),
                                dve_end, [t])

        pe_out, act_end = counter("pe_out"), counter("act_end")

        def out_project(b, w, groups=range(NG), apart=None):
            n = SEQ // P
            for qt in range(n):
                to = apart[qt] if apart else X_BANK
                at = 0 if apart else qt * EMB
                for hg in groups:
                    t = put("pe", lambda e, qt=qt, hg=hg, to=to, at=at: e.matmul(
                        bank(to)[:, at:at + EMB], o_norm[:, hg, qt * P:(qt + 1) * P], w[:, hg],
                        start=(hg == 0), stop=(hg == NG - 1)), pe_out, opt(norm_done[hg], x_free.get(to)))
                if apart and groups[-1] == NG - 1:
                    x_free[to] = put("dve", lambda e, qt=qt, to=to: e.tensor_tensor(
                        x[:, b * n + qt], bank(to)[:, 0:EMB], x[:, b * n + qt], ALU.add), dve_end,
                        [t, setup["bias"]])
            if not apart:
                rows = x[:, b * n:b * n + n]
                x_free[X_BANK] = put("dve", lambda e: e.tensor_tensor(
                    rows, bank(X_BANK).rearrange("p (t c) -> p t c", t=n), rows, ALU.add), dve_end,
                    [t, setup["bias"]])

        def max_free():
            for i in range(2):
                x_free[M_BANKS[i]] = max_used[i]

        def finish_tasks(g):
            b, hg = divmod(g, NG)
            if hg == NG - 2:
                return {V_NORM: lambda: end_norm(hg, bv)}
            if hg < NG - 1:
                return {MAX_STEPS + 1: lambda: end_norm(hg, bv)}
            if g == GROUPS - 1:
                first, last = range(NG - 1), range(NG - 1, NG)
                return {0: lambda: out_project(b, wo, first, M_BANKS), 1: lambda: end_norm(hg, bv),
                        2: lambda: out_project(b, wo, last, M_BANKS)}
            return {FIN_STEPS[0]: lambda: end_norm(hg, bv), FIN_STEPS[1]: lambda: out_project(b, wo)}

        FIRST_K, MID = 0.3, 0.7
        EARLY_FROM = 12
        V_NORM, FIN_STEPS = 1, (28, 31)
        Q_AT = 3
        cross_top, top[0] = top[0], kept
        xn3 = carve((TT, EMB))
        xT3 = carve((KE, SEQ))
        wr = carve((KE, BANKS))
        br = carve((BANKS,))
        b2 = carve((EMB,))
        bank_no = carve((BANKS,))
        tile_size = carve((TT,))
        tile_no = carve((SLOT_TILES,))
        tile_start = carve((SLOT_TILES + 1,))
        row_no = carve((P,))
        pair_high = carve((2 * TT,))
        pair_low = carve((2 * TT,))
        spare_no = carve((SLOT_TILES,))
        before_f = carve((P,))
        before, ones = carve((P,), BF16), carve((P,), BF16)
        logit = carve((TT, BANKS))
        lmax = carve((TT,))
        prob = carve((TT, BANKS))
        psumr = carve((TT,))
        prec = carve((TT,))
        top8 = carve((TT, 8))
        idx8 = carve((TT, 8), U32)
        idxf = carve((TT, 2))
        hot = [carve((TT, BANKS)) for _ in range(2)]
        both = carve((TT, BANKS), BF16)
        earlier = carve((TT + 1, BANKS), BF16)
        routed = top[0]
        assert top[0] <= early_at
        top[0] = early_at
        xn2 = carve((TT, EMB))
        xT2 = carve((KE, TOK))
        wqkv = carve((KE, 3 * EMB))
        wo2 = carve((NG, EMB))
        bqkv = carve((2 * KE,))
        bv2 = carve((NG,))
        bo2 = carve((EMB,))
        wmask = carve((2, WIN))
        hmask = carve((P // HD,))
        q2 = carve((KE, TOK))
        k2 = carve((KE, TOK))
        vals2 = carve((TT, HEADS * VW))
        assert top[0] <= early_at + 2 * GH * KV // 2
        top[0] = early_at + 2 * GH * KV // 2
        qm = carve((HEADS, TOK))
        biased = [carve((GH, WIN)) for _ in range(3)]
        nmax = [carve((GH,)) for _ in range(3)]
        wt2 = [carve((GH, WIN)) for _ in range(3)]
        wTa = [carve((GH * P,)) for _ in range(2)]
        wTb = [carve((GH * P,)) for _ in range(2)]
        top[0] = cross_top

        ld_b, pool_b = counter("ld_b"), counter("pool_b")
        pe_qkv, dve_qkv = counter("pe_qkv"), counter("dve_qkv")
        early_tiles = (BATCH - 1) * (SEQ // P)
        two = {"read": {}}

        def bias2(tiles, rows):
            for i in tiles:
                setup["bias"] = put("pool", lambda e, i=i: e.tensor_tensor(x[:, i], x[:, i], bo2, ALU.add), pool_bias,
                                    [t_wb[0], rows[-1]])

        def early_loads():
            free = [scores_done[GROUPS - 2], (pe_max, pe_max.value)]
            for dst, src in ((wqkv, "w_qkv"), (bqkv, "b_qk"), (bo2, "b_out"), (hmask, "hmask"), (wmask, "wmask"),
                             (bv2, "b_v"), (wo2, "w_out")):
                t_wb[0] = dma("sp", dst, a[src], ld_b, free)
            t_vones2[0] = put("pool", lambda e: e.memset(vals2.rearrange("p t (h w) -> p t h w", w=VW)[:, :, :, HD],
                                                         1.0), pool_b, free)
        def early_norm():
            put("dve", None, None, [scores_done[GROUPS - 2]])
            two["rows"] = all_of(layernorm(xn2, [(dve_end, dve_end.value)], range(early_tiles)))
            bias2(range(early_tiles), two["rows"])

        t_wb, t_vones2 = [None], [None]

        def take_bank(banks):
            xb = banks[0]
            banks.append(banks.pop(0))
            return xb

        def turn_half(half, k, banks):
            xb = take_bank(banks)
            for j in range(TT // 2):
                i = half * (TT // 2) + j
                t = put("pe", lambda e, i=i, j=j: e.transpose(
                    bank(xb)[:, j * P:(j + 1) * P], xn2[:, i, k * P:(k + 1) * P], identf), pe_lnT,
                    opt(*two["rows"], x_free.get(xb)))
            x_free[xb] = two["xT", half] = put("dve", lambda e: e.tensor_copy(
                xT2[:, k, half * CH:(half + 1) * CH], bank(xb)), dve_qkv, [t])

        def project_qk(half, m, banks):
            xb = take_bank(banks)
            for k in range(KE):
                t = put("pe", lambda e, k=k: e.matmul(
                    bank(xb), wqkv[:, k, m * P:(m + 1) * P], xT2[:, k, half * CH:(half + 1) * CH],
                    start=(k == 0), stop=(k == KE - 1)), pe_qkv, opt(two["xT", half], t_wb[0], x_free.get(xb)))
            to = (q2 if m < KE else k2)[:, m % KE, half * CH:(half + 1) * CH]
            sc = QSCALE if m < KE else 1.0
            x_free[xb] = two["qk", half] = put("dve", lambda e: e.tensor_scalar(
                to, bank(xb), bqkv[:, m:m + 1], sc, ALU.add, ALU.mult), dve_qkv, [t])
            if half and m < KE:
                mask_heads(half, m)

        def project_v2(i, banks):
            xb = take_bank(banks)
            dst = bank(xb)[:, 0:EMB]
            half = i // (TT // 2)
            for k in range(KE):
                t = put("pe", lambda e, k=k: e.matmul(
                    dst, xT2[:, k, i * P:(i + 1) * P], wqkv[:, k, 2 * EMB:3 * EMB],
                    start=(k == 0), stop=(k == KE - 1)), pe_qkv, opt(two["xT", half], t_wb[0], x_free.get(xb)))
            x_free[xb] = two["v", half] = put("dve", lambda e: e.tensor_copy(
                vals2[:, i].rearrange("p (h w) -> p h w", w=VW)[:, :, 0:HD],
                dst.rearrange("p (h w) -> p h w", w=HD)), dve_qkv, [t, t_vones2[0]])

        def mask_heads(half, m):
            n = P // HD
            sl = slice(half * CH, (half + 1) * CH)
            for j in range(n):
                two["mask", half, m] = put(*(("pool", "dve")[half == 0], lambda e, j=j: e.tensor_scalar_mul(
                    qm[:, m * n + j, sl], q2[:, m, sl], hmask[:, j:j + 1]), (pool_b, dve_qkv)[half == 0]),
                    [two["qk", half], t_wb[0]] + late)

        UNITS = BATCH * NG * 2
        late = []

        def half_tasks(half, banks):
            return ([lambda k=k: turn_half(half, k, banks) for k in range(KE)]
                    + [lambda m=m: project_qk(half, m, banks) for m in range(2 * KE)]
                    + [lambda i=i: project_v2(i, banks) for i in range(half * TT // 2, (half + 1) * TT // 2)])

        MAX_STEPS = 28
        K_STEPS = [1, 4, 6, 9, 11, 14, 16, 19]
        MAXES = GH * 2 * NCH
        for s in range(-2, GROUPS + 1):
            nxt = s + 1
            if s % 2 != 0 and s + 2 < GROUPS:
                scatter_k(s + 2)
            if 0 <= s and s + 2 < GROUPS:
                load_q(s + 2)
            if s == -2:
                normalise()
                for c in range(NCH):
                    project_k(0, c)
                    if len(later) > 1:
                        later.pop(0)()
                    if c == Q_AT:
                        project_q(0)
                        load_q(0)
                        load_q(1)
                while later:
                    later.pop(0)()
                project_q(1)
                end_setup()
                continue
            todo = finish_tasks(s - 1) if s >= 1 else {}
            with_k = s % 2 == 0 and (s + 2) // 2 < GROUPS // 2
            with_v = s % NG == NG - 1 and (s + 1) // NG < BATCH
            spent, work = [], 0.0
            for t_ in range(MAX_STEPS):
                work += (0.93 if s >= 0 else 0.01) + 1.5 * (with_k and t_ in K_STEPS) + 0.86 * (with_v and t_ > 1)
                spent.append(work)
            spent += [work] * (KT + 2 - MAX_STEPS)
            given = 0

            def maxes(share):
                nonlocal given
                while 0 <= nxt < GROUPS and given < min(MAXES, int(MAXES * share) + 1):
                    max_task(nxt, given)
                    given += 1

            for t_ in range(KT + 2):
                if 0 <= s < GROUPS and t_ < KT:
                    scores(s, t_)
                first = FIRST_K if with_k and t_ in K_STEPS else 0.5
                maxes((first * spent[t_] + (1 - first) * (spent[t_ - 1] if t_ else 0.0)) / spent[-1])
                while later:
                    later.pop()()
                if t_ == MAX_STEPS and 0 <= nxt < GROUPS:
                    max_end(nxt)
                if t_ == MAX_STEPS + 2 and 0 <= nxt < GROUPS:
                    max_rows(nxt)
                if t_ > 1 and 0 <= s < GROUPS:
                    weigh(s, t_ - 2)
                if with_k and t_ in K_STEPS:
                    c = K_STEPS.index(t_)
                    since, till = spent[t_ - 1] if t_ else 0.0, spent[t_]
                    project_k((s + 2) // 2, c, lambda: maxes((since + MID * (till - since)) / spent[-1]))
                maxes(spent[t_] / spent[-1])
                if t_ in todo:
                    todo[t_]()
                if s == GROUPS - 1:
                    if t_ == 0:
                        max_free()
                        early_loads()
                    if t_ == V_NORM:
                        early_norm()
                        early = half_tasks(0, list(M_BANKS))
                    if t_ >= EARLY_FROM and t_ % 3 != 0 and early:
                        early.pop(0)()
                if with_v and t_ > 1:
                    project_v((s + 1) // NG, t_ - 2)
            if s == GROUPS - 1:
                fresh = phase_end()
                late += fresh
                mask_heads(0, 0)
            if 0 <= s < GROUPS:
                end_copy(pv_done[-1])

        ld_c = counter("ld_c")
        for dst, src in ((wr, "Wr"), (br, "br"), (b2[0:BANKS], "b2"), (bank_no, "bank_no"),
                         (tile_size, "tile_size"), (tile_no, "tile_no"), (tile_start, "tile_start"),
                         (row_no, "row_no"), (pair_high, "pair_high"), (pair_low, "pair_low"), (spare_no, "spare_no"),
                         (before_f, "before")):
            t_wc = dma("sp", dst, a[src], ld_c, fresh)
        last_tiles = range(early_tiles, TT)
        statistics, root, apply = layernorm(xn2, [(dve_end, dve_end.value)], last_tiles)

        def apply_last():
            root()
            two["rows"] = apply()
            bias2(last_tiles, two["rows"])

        behind = [lambda: mask_heads(0, 1), statistics, apply_last] + half_tasks(1, [X_BANK])
        PER_UNIT = 1

        for i in range(2):
            t_edge = put("pool", lambda e, i=i: e.memset(wTb[i], 0.0), pool_b, fresh + [(pool_b, pool_b.value)])

        def qkv_done(u):
            half, m = u // (UNITS // 2), (u // 2) % NG // 2
            return ([two["qk", half], two["v", half], t_vones2[0]]
                    + [two["mask", half, m]])

        pe_s2, dve_s2, act_s2, pe_t2, act_t2, pe_v2 = (counter(n) for n in (
            "pe_s2", "dve_s2", "act_s2", "pe_t2", "act_t2", "pe_v2"))
        s_read = exp_done[-2:]
        t_read = [x_free[M_BANKS[0]], x_free[M_BANKS[1]]]
        w_read = [None] * 3
        wT_read = [None, None]
        soft = {}

        def softmax2(u):
            b, hg, qt = u // 8, (u // 2) % 4, u % 2
            i, r = u % 2, u % 3
            at = b * SEQ + qt * (SEQ - WIN)
            tok = b * SEQ + qt * P
            dst = bank(2 * i, 2).rearrange("p (h w) -> p h w", h=GH)[:, :, 0:WIN]
            for j in range(GH):
                h = hg * GH + j
                t = put("pe", lambda e, j=j, h=h: e.matmul(
                    dst[:, j], qm[:, h, tok:tok + P], k2[:, h // (P // HD), at:at + WIN], start=True, stop=True),
                    pe_s2, opt(s_read[i]) + qkv_done(u))
            s_read[i] = t = put("dve", lambda e: e.tensor_tensor(
                biased[r], dst, wmask[:, qt:qt + 1].broadcast_to([P, GH, WIN]), ALU.add), dve_s2, opt(t, w_read[r]))
            t = put("dve", lambda e: e.tensor_reduce(nmax[r], biased[r], AX_X, ALU.max, negate=True), dve_s2, [t])
            for j in range(GH):
                t2 = put("act", lambda e, j=j: e.activation(wt2[r][:, j], biased[r][:, j], ACT.Exp,
                                                            bias=nmax[r][:, j:j + 1]), act_s2, opt(t, w_read[r]))
            soft[u] = t2

        def halves(u):
            b, qt = u // 8, u % 2
            full_at, edge_at, lo = ((0, P, 0), (HALF, 0, P - HALF))[qt]
            return full_at, edge_at, lo, 2 * b + qt, 2 * b + 1 - qt

        wT_done = {}

        def turn2(u):
            i, r = u % 2, u % 3
            full_at, edge_at, lo, _, _ = halves(u)
            for j in range(GH):
                ta = put("pe", lambda e, j=j: e.transpose(bank(4)[:, j * P:(j + 1) * P],
                                                          wt2[r][:, j, full_at:full_at + P], identf),
                         pe_t2, opt(soft[u], t_read[0]))
            for j in range(GH):
                tb = put("pe", lambda e, j=j: e.matmul(bank(5)[lo:lo + HALF, j * P:(j + 1) * P],
                                                       wt2[r][:, j, edge_at:edge_at + HALF],
                                                       identf, start=True, stop=True), pe_t2, opt(t_read[1]))
            w_read[r] = tb
            t_read[0] = put("act", lambda e: e.activation(wTa[i], bank(4), ACT.Copy), act_t2, opt(ta, wT_read[i]))
            t_read[1] = put("act", lambda e: e.activation(wTb[i][lo:lo + HALF], bank(5)[lo:lo + HALF], ACT.Copy),
                            act_t2, opt(tb, wT_read[i], t_edge))
            wT_done[u] = (t_read[0], t_read[1])

        def weigh2(u):
            b, hg, qt = u // 8, (u // 2) % 4, u % 2
            i = u % 2
            _, _, _, ft, et = halves(u)
            o = bank(O_BANK)
            for j in range(GH):
                h = hg * GH + j
                put("pe", lambda e, j=j, h=h: e.matmul(
                    o[32 * j:32 * j + VW, qt * P:(qt + 1) * P], vals2[:, ft, h * VW:(h + 1) * VW],
                    wTa[i][:, j * P:(j + 1) * P], start=True, stop=False), pe_v2,
                    opt(wT_done[u][0], o_read[0]) + qkv_done(u))
            for j in range(GH):
                h = hg * GH + j
                t = put("pe", lambda e, j=j, h=h: e.matmul(
                    o[32 * j:32 * j + VW, qt * P:(qt + 1) * P], vals2[:, et, h * VW:(h + 1) * VW],
                    wTb[i][:, j * P:(j + 1) * P], start=False, stop=True), pe_v2, [wT_done[u][1]])
            wT_read[i] = t
            if qt == 1:
                end_copy(t)

        def finish2(u):
            b, hg, qt = u // 8, (u // 2) % 4, u % 2
            if u == UNITS - 1:
                x_free[S_BANKS[0]], x_free[S_BANKS[1]] = s_read
                out_project(b, wo2, range(NG - 1), S_BANKS)
            if qt == 1:
                end_norm(hg, bv2)

        def project2(u):
            b, hg, qt = u // 8, (u // 2) % 4, u % 2
            if qt == 1 and hg == NG - 1:
                if b < BATCH - 1:
                    out_project(b, wo2)
                else:
                    out_project(b, wo2, range(NG - 1, NG), S_BANKS)

        pe_r, dve_r, act_r = counter("pe_r"), counter("dve_r"), counter("act_r")
        st_rows = counter("st_rows")
        t_none = put("pool", lambda e: e.memset(earlier[:, 0], 0.0), pool_b, fresh + [(pool_b, pool_b.value)])
        t_ones16 = put("pool", lambda e: e.memset(ones, 1.0), pool_b, fresh + [(pool_b, pool_b.value)])
        t_before = put("pool", lambda e: e.tensor_copy(before, before_f), pool_b, [t_wc, (pool_b, pool_b.value)])

        def over_tiles(v, n=TT):
            return v.rearrange("p (o e) -> p o e", o=1).broadcast_to([P, n, BANKS])

        def over_banks(v, n=TT):
            return v.rearrange("p (t o) -> p t o", o=1).broadcast_to([P, n, BANKS])

        def router(batches):
            n = SEQ // P
            tiles = range(batches[0] * n, batches[-1] * n + n)
            sl = slice(tiles[0], tiles[-1] + 1)
            nt = len(tiles)
            statistics, root, apply = layernorm(xn3, [(dve_end, dve_end.value)], tiles)
            got = {}

            def normalise3():
                got["rows"] = apply()
                dma("sp", scratch["rows_x"].rearrange("(p i) e -> p i e", i=TT)[:, sl], xn3[:, sl], st_rows,
                    got["rows"])

            def turn3(b):
                dst = bank(X_BANK)
                for k in range(KE):
                    for j in range(n):
                        t = put("pe", lambda e, j=j, k=k: e.transpose(
                            dst[:, (k * n + j) * P:(k * n + j + 1) * P],
                            xn3[:, b * n + j, k * P:(k + 1) * P], identf), pe_r,
                            opt(*got["rows"], x_free[X_BANK]))
                x_free[X_BANK] = got["xT"] = put("act", lambda e: e.activation(
                    xT3.rearrange("p k t -> p (k t)"), dst, ACT.Copy), act_r, [t, (pe_r, pe_r.value)])

            def logits(b):
                dst = bank(X_BANK)[:, 0:n * BANKS]
                for j in range(n):
                    for k in range(KE):
                        t = put("pe", lambda e, j=j, k=k: e.matmul(
                            dst[:, j * BANKS:(j + 1) * BANKS], xT3[:, k, j * P:(j + 1) * P], wr[:, k],
                            start=(k == 0), stop=(k == KE - 1)), pe_r, [got["xT"], x_free[X_BANK], t_wc])
                x_free[X_BANK] = got["lg"] = put("dve", lambda e: e.tensor_tensor(
                    logit[:, b * n:b * n + n], dst.rearrange("p (t e) -> p t e", t=n), over_tiles(br, n), ALU.add),
                    dve_r, [t])

            def subtract():
                lg = logit[:, sl]
                t = put("dve", lambda e: e.reduce_max(lmax[:, sl], lg, AX_X), dve_r, [got["lg"]])
                got["lg"] = put("dve", lambda e: e.tensor_tensor(lg, lg, over_banks(lmax[:, sl], nt), ALU.subtract),
                                dve_r, [t])

            def exponent():
                got["exp"] = put("act", lambda e: e.activation(prob[:, sl], logit[:, sl], ACT.Exp), act_r,
                                 [got["lg"]])

            def choose():
                pr = prob[:, sl]
                t = put("dve", lambda e: e.reduce_sum(psumr[:, sl], pr, AX_X), dve_r, [got["exp"]])
                t = put("dve", lambda e: e.reciprocal(prec[:, sl], psumr[:, sl]), dve_r, [t])
                t = put("dve", lambda e: e.tensor_tensor(pr, pr, over_banks(prec[:, sl], nt), ALU.mult), dve_r, [t])
                t_top = [put("dve", lambda e, i=i: e.max(top8[:, i], prob[:, i]), dve_r, [t]) for i in tiles]
                for i, t in zip(tiles, t_top):
                    t = put("dve", lambda e, i=i: e.max_index(idx8[:, i], top8[:, i], prob[:, i]), dve_r, [t])
                t = put("dve", lambda e: e.tensor_copy(idxf[:, sl], idx8[:, sl, 0:2]), dve_r, [t])
                for c in range(2):
                    t_hot = put("dve", lambda e, c=c: e.tensor_tensor(
                        hot[c][:, sl], over_tiles(bank_no, nt), over_banks(idxf[:, sl, c], nt), ALU.is_equal),
                        dve_r, [t, t_wc])
                t = put("dve", lambda e: e.tensor_tensor(both[:, sl], hot[0][:, sl], hot[1][:, sl], ALU.add),
                        dve_r, [t_hot])
                for i in tiles:
                    t = put("dve", lambda e, i=i: e.tensor_tensor(earlier[:, i + 1], earlier[:, i], both[:, i],
                                                                  ALU.add), dve_r, [t, t_none])
                return t

            projections = [lambda step=step, b=b: step(b) for b in batches for step in (turn3, logits)]
            return [statistics, root, normalise3] + projections + [subtract, exponent, choose]

        ROUTED = (range(0, 2), range(2, 4))
        ROUTING_STEPS = 1
        routing = []
        for u in range(UNITS + 5):
            def run(*steps):
                for lag, step in steps:
                    if 0 <= u - lag < UNITS:
                        step(u - lag)

            run((2, turn2), (3, weigh2))
            if u:
                for step in behind[0:PER_UNIT] + routing[0:ROUTING_STEPS]:
                    step()
                del behind[0:PER_UNIT], routing[0:ROUTING_STEPS]
            assert not behind or u + 1 < UNITS // 2
            run((0, softmax2), (4, finish2), (5, project2))
            for batches in ROUTED:
                if u == 4 + (batches[-1] + 1) * NG * 2:
                    routing += router(batches)
        while routing:
            t_both = routing.pop(0)()

        fresh = phase_end()
        top[0] = routed
        gate = carve((TT, BANKS))
        gtmp = carve((TT, BANKS))
        gT = carve((TOK,))
        cmp = carve((BANKS, TT))
        tiles = carve((BANKS,))
        ends = [carve((BANKS,)) for _ in range(2)]
        start = carve((BANKS,))
        slot_of = carve((TT, BANKS))
        slotf = carve((2 * TT,))
        past = carve((SLOT_TILES, BANKS))
        ownerf = carve((SLOT_TILES,))
        owner = carve((SLOT_TILES,), I32)
        reached = carve((2 * TT, SLOT_TILES + 1))
        at_tile = carve((2 * TT, SLOT_TILES))
        in_tile = [carve((2 * TT, SLOT_TILES), BF16) for _ in range(2)]
        tiles_in = carve((2 * TT,))
        row = carve((2 * TT,))
        at_row = carve((2 * TT, P), BF16)
        pair = carve((SLOT_TILES,))
        spare = carve((SLOT_TILES,))
        second = carve((SLOT_TILES,))
        from_row = carve((SLOT_TILES,), U32)
        to_row = carve((SLOT_TILES,), U32)
        RING = 6
        w1s = [carve((KE, HID)) for _ in range(RING)]
        w2s = [carve((HC, EMB)) for _ in range(RING)]
        b1s = [carve((HC,)) for _ in range(RING)]
        XRING = 5
        xin = [carve((EMB,)) for _ in range(XRING)]
        xTt = [carve((KE, P)) for _ in range(2)]
        hid = [carve((HC, P)) for _ in range(2)]
        yout = [carve((EMB,)) for _ in range(3)]
        picked = carve((2 * TT, EMB))

        by_tile = "p t e -> p (t e)"
        counts = bank(4)[:, 0:BANKS]
        t_counts = put("pe", lambda e: e.matmul(counts, ones, earlier[:, TT], start=True, stop=True), pe_r,
                       [t_both, t_ones16, t_before] + fresh)
        rank = bank(3)[:, 0:TT * BANKS]
        put("pe", lambda e: e.matmul(rank, before, both.rearrange(by_tile), start=True, stop=False), pe_r)
        t_rank = put("pe", lambda e: e.matmul(rank, ones, earlier[:, 0:TT].rearrange(by_tile),
                                              start=False, stop=True), pe_r)
        t = put("dve", lambda e: e.tensor_tensor(
            cmp, counts.rearrange("p (e o) -> p e o", o=1).broadcast_to([P, BANKS, TT]),
            tile_size.rearrange("p (o t) -> p o t", o=1).broadcast_to([P, BANKS, TT]), ALU.is_gt), dve_r, [t_counts])
        t = put("dve", lambda e: e.reduce_sum(tiles, cmp, AX_X), dve_r, [t])
        src = tiles
        for n, d in enumerate((1, 2, 4, 8)):
            dst = ends[n % 2]
            put("dve", lambda e, src=src, dst=dst, d=d: e.tensor_copy(dst[:, 0:d], src[:, 0:d]), dve_r, [t])
            t = put("dve", lambda e, src=src, dst=dst, d=d: e.tensor_tensor(
                dst[:, d:], src[:, d:], src[:, 0:BANKS - d], ALU.add), dve_r, [t])
            t = (dve_r, dve_r.value)
            src = dst
        t_ends, last_tile = t, src
        t = put("dve", lambda e: e.tensor_tensor(start, last_tile, tiles, ALU.subtract), dve_r, [t])
        t_start = put("dve", lambda e: e.tensor_scalar_mul(start, start, float(P)), dve_r, [t])
        t = put("dve", lambda e: e.tensor_tensor(
            past[0:1], last_tile[0:1].rearrange("p (o e) -> p o e", o=1).broadcast_to([1, SLOT_TILES, BANKS]),
            tile_no[0:1].rearrange("p (j o) -> p j o", o=1).broadcast_to([1, SLOT_TILES, BANKS]), ALU.is_le),
            dve_r, [t_ends])
        t = put("dve", lambda e: e.reduce_sum(ownerf[0:1], past[0:1], AX_X), dve_r, [t])
        t_owner = put("dve", lambda e: e.tensor_scalar_min(owner[0:1], ownerf[0:1], float(BANKS - 1)), dve_r, [t])
        t = put("dve", lambda e: e.tensor_tensor(slot_of, rank.rearrange("p (t e) -> p t e", t=TT),
                                                 over_tiles(start), ALU.add), dve_r, [t_start, t_rank])
        for c in range(2):
            t = put("dve", lambda e, c=c: e.tensor_tensor(gtmp, slot_of, hot[c], ALU.mult), dve_r, [t])
            t = put("dve", lambda e, c=c: e.reduce_sum(slotf[:, c * TT:(c + 1) * TT], gtmp, AX_X), dve_r, [t])
        def spread_pairs(v, n):
            return v.rearrange("p (t o) -> p t o", o=1).broadcast_to([P, 2 * TT, n])

        def spread_row(v, n):
            return v.rearrange("p (o n) -> p o n", o=1).broadcast_to([P, 2 * TT, n])

        t = put("dve", lambda e: e.tensor_tensor(reached, spread_pairs(slotf, SLOT_TILES + 1),
                                                 spread_row(tile_start, SLOT_TILES + 1), ALU.is_ge), dve_r, [t])
        t2 = put("dve", lambda e: e.tensor_tensor(at_tile, reached[:, :, 0:SLOT_TILES], reached[:, :, 1:],
                                                  ALU.subtract), dve_r, [t])
        for part, number in enumerate((pair_high, pair_low)):
            t_in = put("dve", lambda e, part=part, number=number: e.tensor_tensor(
                in_tile[part], at_tile, spread_pairs(number, SLOT_TILES), ALU.mult), dve_r, [t2])
        t_in = (dve_r, dve_r.value)
        t = put("dve", lambda e: e.reduce_sum(tiles_in, reached, AX_X), dve_r, [t])
        t = put("dve", lambda e: e.scalar_tensor_tensor(row, tiles_in, -float(P), slotf, ALU.mult, ALU.add),
                dve_r, [t])
        t = put("dve", lambda e: e.tensor_tensor(at_row, spread_pairs(row, P), spread_row(row_no, P), ALU.is_equal),
                dve_r, [t])
        of_slot = bank(5)[:, 0:SLOT_TILES]
        for n in range(2 * TT):
            for part in range(2):
                t_pair = put("pe", lambda e, n=n, part=part: e.matmul(
                    of_slot, at_row[:, n], in_tile[part][:, n], start=(n + part == 0),
                    stop=(n + part == 2 * TT)), pe_r, [t, t_in])
        t_pair = put("dve", lambda e: e.tensor_copy(pair, of_slot), dve_r, [t_pair])
        t = put("dve", lambda e: e.tensor_scalar(second, pair, TOK + 0.5, float(TOK), ALU.is_gt, ALU.mult), dve_r,
                [t_pair])
        t = put("dve", lambda e: e.scalar_tensor_tensor(second, pair, -1.0, second, ALU.add, ALU.subtract), dve_r, [t])
        t_from = put("dve", lambda e: e.tensor_scalar_max(from_row, second, 0.0), dve_r, [t])
        t = put("dve", lambda e: e.scalar_tensor_tensor(spare, pair, 0.0, spare_no, ALU.is_equal, ALU.mult), dve_r,
                [t_pair])
        t_to = put("dve", lambda e: e.scalar_tensor_tensor(to_row, pair, -1.0, spare, ALU.add, ALU.add), dve_r, [t])
        t = put("dve", lambda e: e.tensor_tensor(gate, hot[0], over_banks(top8[:, :, 0]), ALU.mult), dve_r)
        t = put("dve", lambda e: e.tensor_tensor(gtmp, hot[1], over_banks(top8[:, :, 1]), ALU.mult), dve_r, [t])
        t_gate = put("dve", lambda e: e.tensor_tensor(gate, gate, gtmp, ALU.add), dve_r, [t])

        ld_w12 = [counter(f"ld_w12{i}") for i in range(RING)]
        ld_x = [counter(f"ld_x{i}") for i in range(XRING)]
        pe_x, act_x, pe_h, act_h, dve_h, pe_y, dve_y = (counter(n) for n in (
            "pe_x", "act_x", "pe_h", "act_h", "dve_h", "pe_y", "dve_y"))
        st_y = [counter(f"st_y{i}") for i in range(3)]
        rows_stored = (st_rows, st_rows.value)
        w_in, x_in, xT_in, h_in, y_out = {}, {}, {}, {}, {}
        turned, up_pe, down_pe = {}, {}, {}

        def load_tile(j, after=()):
            i = j % RING

            def weights(e):
                owns = e.value_load(owner[0:1, j:j + 1], min_val=0, max_val=BANKS - 1)
                e.dma_start(w1s[i], a["W1"][bass.ds(owns, 1)].rearrange("o p k n -> p (o k) n")).then_inc(
                    ld_w12[i].sem, 16)
                e.dma_start(w2s[i], a["W2"][bass.ds(owns, 1)].rearrange("o p k n -> p (o k) n")).then_inc(
                    ld_w12[i].sem, 16)
                return e.dma_start(b1s[i], a["b1"][bass.ds(owns, 1)].rearrange("o p k -> p (o k)"))

            ld_w12[i].value += 32
            w_in[j] = put("sp", weights, ld_w12[i], opt(t_owner, down_pe.get(j - RING), *after), 16)

        def load_rows(j):
            i = j % XRING
            x_in[j] = put("pool", lambda e: e.indirect_dma_start(
                xin[i], None, scratch["rows_x"], bass.IndirectOffsetOnAxis(ap=from_row[:, j:j + 1], axis=0)),
                ld_x[i], opt(t_from, rows_stored, turned.get(j - XRING)), 16)

        def turn(j):
            dst = bank(6 + j % 2)[:, 0:KE * P]
            for k in range(KE):
                t = put("pe", lambda e, k=k: e.transpose(dst[:, k * P:(k + 1) * P],
                                                         xin[j % XRING][:, k * P:(k + 1) * P], identf), pe_x,
                        opt(x_in[j], xT_in.get(j - 2)))
            turned[j] = t
            xT_in[j] = put("dve", lambda e: e.tensor_copy(xTt[j % 2].rearrange("p k t -> p (k t)"), dst), act_x,
                           opt(t, up_pe.get(j - 2)))

        def up(j):
            for hb in range(2):
                dst = bank(2 * (j % 2) + hb)
                for q in range(HC // 2):
                    hc = hb * (HC // 2) + q
                    for k in range(KE):
                        t = put("pe", lambda e, k=k, q=q, hc=hc, dst=dst: e.matmul(
                            dst[:, q * P:(q + 1) * P], w1s[j % RING][:, k, hc * P:(hc + 1) * P], xTt[j % 2][:, k],
                            start=(k == 0), stop=(k == KE - 1)), pe_h,
                            opt(w_in[j], xT_in[j], *h_in.get(j - 2, ())))
                ws = opt(t, down_pe.get(j - 2))
                for q in range(HC // 2):
                    hc = hb * (HC // 2) + q
                    src = dst[:, q * P:(q + 1) * P]
                    if hb:
                        t_d = put("dve", lambda e, hc=hc, src=src: e.tensor_scalar(
                            hid[j % 2][:, hc], src, b1s[j % RING][:, hc:hc + 1], 0.0, ALU.add, ALU.max), dve_h, ws)
                    else:
                        t_a = put("act", lambda e, hc=hc, src=src: e.activation(
                            hid[j % 2][:, hc], src, ACT.Relu, bias=b1s[j % RING][:, hc:hc + 1]), act_h, ws)
            up_pe[j] = t
            h_in[j] = (t_a, t_d)

        def down(j):
            dst = bank(4 + j % 2)[:, 0:EMB]
            for hc in range(HC):
                t = put("pe", lambda e, hc=hc: e.matmul(dst, hid[j % 2][:, hc], w2s[j % RING][:, hc],
                                                        start=(hc == 0), stop=(hc == HC - 1)), pe_y,
                        opt(*h_in[j], y_out.get(j - 2)))
            down_pe[j] = t
            i = j % 3
            y_out[j] = put("dve", lambda e: e.tensor_copy(yout[i], dst), dve_y,
                           opt(t, (st_y[i], st_y[i].value)))
            put("pool", lambda e: e.indirect_dma_start(
                scratch["rows_y"], bass.IndirectOffsetOnAxis(ap=to_row[:, j:j + 1], axis=0), yout[i], None),
                st_y[i], [y_out[j], t_to], 16)

        for j in range(3):
            load_rows(j)
        for j in range(RING):
            load_tile(j, [x_in[1]] if j > 1 else [])
        for s in range(SLOT_TILES + 2):
            if s < SLOT_TILES:
                turn(s)
                if s + 3 < SLOT_TILES:
                    load_rows(s + 3)
            if 1 <= s < SLOT_TILES + 1:
                up(s - 1)
            if s >= 2:
                down(s - 2)
                if s - 2 + RING < SLOT_TILES:
                    load_tile(s - 2 + RING)

        for i in range(TT):
            t = put("pe", lambda e, i=i: e.matmul(bank(i // 4)[0:BANKS, (i % 4) * P:(i % 4 + 1) * P], gate[:, i],
                                                  identf, start=True, stop=True), pe_r,
                    [t_gate, (act_h, act_h.value), (dve_h, dve_h.value)])
        t_gT = put("dve", lambda e: e.tensor_copy(gT[0:BANKS], bank(0, 2)[0:BANKS]), dve_r, [t])
        pe_o, dve_o, st_o = counter("pe_o"), counter("dve_o"), counter("st_o")
        b_read = [None, None]
        for i in range(TT):
            dst = bank(2 + i % 2)[:, 0:EMB]
            t = put("pe", lambda e, i=i, dst=dst: e.matmul(dst, gT[0:BANKS, i * P:(i + 1) * P], b2[0:BANKS],
                                                           start=True, stop=True), pe_o,
                    opt(t_gT, b_read[i % 2]))
            b_read[i % 2] = put("dve", lambda e, i=i, dst=dst: e.tensor_tensor(x[:, i], dst, x[:, i], ALU.add),
                                dve_o, [t])

        written = [(c, c.value) for c in st_y]
        ld_y = [counter(f"ld_y{b}") for b in range(BATCH)]
        by_pair = scratch["rows_y"][0:2 * TOK].rearrange("(c p i) e -> p c i e", c=2, i=TT)
        n = SEQ // P
        t_y = {}
        for b in range(BATCH):
            for c in range(2):
                t_y[b] = dma(("sp", "act")[c], picked[:, c * TT + b * n:c * TT + b * n + n],
                          by_pair[:, c, b * n:b * n + n], ld_y[b], written)
        for b in range(BATCH):
            for i in range(b * n, b * n + n):
                t = b_read[i % 2]
                for c in range(2):
                    t = put("dve", lambda e, i=i, c=c: e.scalar_tensor_tensor(
                        x[:, i], picked[:, c * TT + i], top8[:, i, c:c + 1], x[:, i], ALU.mult, ALU.add),
                        dve_o, [t, t_y[b]])
            dma("sp", out[:, b * n:b * n + n], x[:, b * n:b * n + n], st_o, [t])
        put("sp", None, None, [(st_o, st_o.value)])

        block = ctx.enter_context(nc.Block())

        def play(name, e):
            for waits, make, sem, by in queue[name]:
                for s, v in waits:
                    e.wait_ge(s, v)
                if make is not None:
                    i = make(e)
                    if sem is not None:
                        i.then_inc(sem, by)

        @block.tensor
        def _(e):
            play("pe", e)

        @block.scalar
        def _(e):
            play("act", e)

        @block.vector
        def _(e):
            play("dve", e)

        @block.gpsimd
        def _(e):
            play("pool", e)

        @block.sync
        def _(e):
            play("sp", e)


def layouts(i):
    f = np.float32

    def rows(w, k, p=P):
        return np.ascontiguousarray(w.reshape(k, p, -1).transpose(1, 0, 2))

    def by_head(w):
        w = w.reshape(NG, GH, HD, -1)
        o = np.zeros((NG, GH, 32, w.shape[-1]), f)
        o[:, :, :HD] = w
        return np.ascontiguousarray(o.reshape(NG, P, -1).transpose(1, 0, 2))

    def by_dim(w):
        return np.ascontiguousarray(w.reshape(NG, GH, HD, -1).swapaxes(1, 2)).reshape(w.shape)

    def spread(v):
        return np.ascontiguousarray(np.broadcast_to(v, (P,) + v.shape))

    q = np.arange(P)[:, None, None]
    j = np.arange(WIN)[None, None, :]
    t = np.arange(2)[None, :, None]
    dist = np.abs(P * t + q - ((SEQ - WIN) * t + j))
    p = np.arange(P)
    bqkv = i["L0_attn_b_qkv"]
    return {
        "x": rows(i["x"].reshape(TOK, EMB), TT),
        "ctxT": np.ascontiguousarray(i["ctx_768"].reshape(BATCH, KV, 2, KC).transpose(0, 3, 2, 1)),
        "wqT": rows(i["L0_xattn_wq"].T, KE),
        "wkT": rows(by_dim(i["L0_xattn_wk"]).T, 2, KC),
        "wvT": rows(i["L0_xattn_wv"].T, 2, KC),
        "woT": by_head(i["L0_xattn_wo"].T),
        "bq": np.ascontiguousarray(i["L0_xattn_bq"].reshape(KE, P).T),
        "bk": np.ascontiguousarray(by_dim(i["L0_xattn_bk"]).reshape(KE, P).T),
        "bv": by_head(i["L0_xattn_bv"])[:, :, 0].copy(),
        "bo": spread(i["L0_xattn_bo"]),
        "w_qkv": rows(i["L0_attn_w_qkv"], KE),
        "w_out": by_head(i["L0_attn_w_out"]),
        "b_qk": np.ascontiguousarray(bqkv[:2 * EMB].reshape(2 * KE, P).T),
        "b_v": by_head(bqkv[2 * EMB:])[:, :, 0].copy(),
        "b_out": spread(i["L0_attn_b_out"]),
        "Wr": rows(i["L0_ffn_Wr"], KE),
        "br": spread(i["L0_ffn_br"]),
        "W1": np.ascontiguousarray(i["L0_ffn_W1"].reshape(BANKS, KE, P, HID).transpose(0, 2, 1, 3)),
        "b1": np.ascontiguousarray(i["L0_ffn_b1"].reshape(BANKS, HC, P).transpose(0, 2, 1)),
        "W2": np.ascontiguousarray(i["L0_ffn_W2"].reshape(BANKS, HC, P, EMB).transpose(0, 2, 1, 3)),
        "b2": i["L0_ffn_b2"],
        "identf": np.eye(P, dtype=f),
        "lsel": (p[:, None] == (p[None, :] // 32) * 32 + HD).astype(f),
        "wmask": np.where(dist <= HALF, f(0), f(-3e38)).astype(f),
        "hmask": (p[:, None] // HD == np.arange(P // HD)[None, :]).astype(f),
        "bank_no": spread(np.arange(BANKS, dtype=f)),
        "tile_size": spread(P * np.arange(TT, dtype=f)),
        "tile_no": spread(np.arange(SLOT_TILES, dtype=f)),
        "tile_start": spread(P * np.arange(SLOT_TILES + 1, dtype=f)),
        "row_no": spread(np.arange(P, dtype=f) - P),
        "pair_high": (TOK * (np.arange(2 * TT)[None, :] // TT) + TT * p[:, None]).astype(f),
        "pair_low": spread((1 + np.arange(2 * TT) % TT).astype(f)),
        "spare_no": (2 * TOK + 1 + p[:, None] + P * np.arange(SLOT_TILES)[None, :]).astype(f),
        "before": (p[:, None] < p[None, :]).astype(f),
    }


def kernel(**inputs):
    import concourse.bacc as bacc
    from concourse.bass_utils import run_bass_kernel_spmd

    nc = bacc.Bacc("TRN2", target_bir_lowering=False, num_devices=1)
    arrays, aps = {}, {}
    for name, v in layouts({k: np.asarray(v) for k, v in inputs.items()}).items():
        arrays[f"in_{name}"] = v
        aps[name] = nc.dram_tensor(f"in_{name}", v.shape, mybir.dt.from_np(v.dtype), kind="ExternalInput").ap()
    out = nc.dram_tensor("out", (P, TT, EMB), F32, kind="ExternalOutput").ap()
    scratch = {"qparts": nc.dram_tensor("qparts", (3, EMB, TOK), BF16, kind="Internal").ap()}
    for name, n in (("rows_x", TOK), ("rows_y", 2 * TOK + SLOT_TILES * P)):
        scratch[name] = nc.dram_tensor(name, (n, EMB), F32, kind="Internal").ap()
    build(nc, aps, out, scratch)
    r = run_bass_kernel_spmd(nc, [arrays], core_ids=[0])
    return np.ascontiguousarray(r.results[0]["out"].transpose(1, 0, 2)).reshape(BATCH, SEQ, EMB)
```
